# Optimizing a Trainium2 kernel written in Bass

```python
import numpy as np
import jax
import jax.numpy as jnp

def _softmax(x, axis=-1):
    return jax.nn.softmax(x, axis=axis)

def _gelu(x):
    return jax.nn.gelu(x, approximate=True)

def _silu(x):
    return jax.nn.silu(x)

def _sigmoid(x):
    return jax.nn.sigmoid(x)

def _layernorm(x, axis=-1, eps=1e-05):
    m = jnp.mean(x, axis=axis, keepdims=True)
    v = jnp.var(x, axis=axis, keepdims=True)
    return (x - m) / jnp.sqrt(v + eps)

def _scatter_add(tgt, idx, src, axis=0):
    return tgt.at[idx].add(src)

def _segment_sum(src, seg, n):
    return jax.ops.segment_sum(src, seg, n)
kernel_name = 'mk_gnn_preln_d1_gnn_r64_1d95f7'

def setup_inputs(seed: int=0):
    np.random.seed(seed)
    _w = jnp.asarray

    def _rec_inputs():
        import jax
        import jax.numpy as jnp
        _gk = jax.random.key(seed)
        x = -0.0009044 + 1 * jax.random.normal(jax.random.fold_in(_gk, 1), (100000, 32), jnp.float32)
        src = jax.random.randint(jax.random.fold_in(_gk, 2), (25000,), 0, 100000, jnp.int32)
        dst = jnp.minimum((100000 * jax.random.uniform(jax.random.fold_in(_gk, 3), (25000,)) ** 2.0).astype(jnp.int32), 99999)
        _o = jnp.argsort(dst, stable=True)
        src = src[_o]
        dst = dst[_o]
        edge_attr3_2x32 = -8.16379e-05 + 0.999858 * jax.random.normal(jax.random.fold_in(_gk, 12), (25000, 2, 32), jnp.float32)
        return (x, src, dst, edge_attr3_2x32)
    x, src, dst, edge_attr3_2x32 = _rec_inputs()

    def _L0_gnn_setup():
        import jax, jax.numpy as jnp
        import numpy as np
        N = 50000
        E = 25000
        H = 2
        F = 32
        IN = 32
        OUT = 32
        NEG_SLOPE = 0.2
        key = jax.random.key(seed)
        ks = jax.random.split(key, 11)
        s = 0.1
        return {'feat': jax.random.normal(ks[0], (N, IN), jnp.float32), 'r_feat': jax.random.normal(ks[1], (E, H, F), jnp.float32), 'src': jax.random.randint(ks[2], (E,), 0, N), 'dst': jax.random.randint(ks[3], (E,), 0, N), 'W1': jax.random.normal(ks[4], (IN, OUT), jnp.float32) * s, 'b1': jnp.zeros((OUT,), jnp.float32), 'W2s': jax.random.normal(ks[5], (IN, H * F), jnp.float32) * s, 'b2s': jnp.zeros((H * F,), jnp.float32), 'W2d': jax.random.normal(ks[6], (IN, H * F), jnp.float32) * s, 'b2d': jnp.zeros((H * F,), jnp.float32), 'attn': jax.random.normal(ks[7], (1, H, F), jnp.float32) * s}
    _L0_gnn_all = _L0_gnn_setup()
    _L0_gnn_in = {k: v for k, v in _L0_gnn_all.items() if k in ('W1', 'b1', 'W2s', 'b2s', 'W2d', 'b2d', 'attn')}
    del _L0_gnn_all
    return {'x': x, 'src': src, 'dst': dst, 'edge_attr3_2x32': edge_attr3_2x32, 'L0_gnn_W1': _L0_gnn_in['W1'], 'L0_gnn_b1': _L0_gnn_in['b1'], 'L0_gnn_W2s': _L0_gnn_in['W2s'], 'L0_gnn_b2s': _L0_gnn_in['b2s'], 'L0_gnn_W2d': _L0_gnn_in['W2d'], 'L0_gnn_b2d': _L0_gnn_in['b2d'], 'L0_gnn_attn': _L0_gnn_in['attn']}

def reference(x, src, dst, edge_attr3_2x32, L0_gnn_W1, L0_gnn_b1, L0_gnn_W2s, L0_gnn_b2s, L0_gnn_W2d, L0_gnn_b2d, L0_gnn_attn):
    import jax
    import jax.numpy as jnp

    def _L0_gnn_ref(feat, r_feat, src, dst, W1, b1, W2s, b2s, W2d, b2d, attn):
        import jax, jax.numpy as jnp
        import numpy as np
        N = 50000
        E = 25000
        H = 2
        F = 32
        IN = 32
        OUT = 32
        NEG_SLOPE = 0.2
        n = feat.shape[0]
        feat_src = (feat @ W2s + b2s).reshape(n, H, F)
        feat_dst = (feat @ W2d + b2d).reshape(n, H, F)
        en = feat_src[src]
        ev = feat_dst[dst]
        e = jax.nn.leaky_relu(en + ev, negative_slope=NEG_SLOPE)
        e = jnp.sum(e * attn, axis=-1, keepdims=True)
        m = jax.ops.segment_max(e, dst, num_segments=n)
        m = jnp.where(jnp.isfinite(m), m, 0.0)
        ee = jnp.exp(e - m[dst])
        denom = jax.ops.segment_sum(ee, dst, num_segments=n)
        alpha = ee / jnp.maximum(denom[dst], 1e-09)
        msg = jax.nn.softmax(en * r_feat * alpha, axis=-1)
        g_agg = jax.ops.segment_sum(msg, dst, num_segments=n)
        g_sum = jnp.sum(g_agg, axis=1)
        rst = (feat + g_sum) @ W1 + b1
        return rst
    h = jnp.maximum(_layernorm(x, axis=-1), 0.0)
    x = x + _L0_gnn_ref(h, edge_attr3_2x32, src, dst, L0_gnn_W1, L0_gnn_b1, L0_gnn_W2s, L0_gnn_b2s, L0_gnn_W2d, L0_gnn_b2d, L0_gnn_attn)
    return x

_drawn_inputs = setup_inputs


def setup_inputs(seed=0):
    import zlib

    import numpy as np

    out = dict(_drawn_inputs(seed))
    spreads = {'L0_gnn_b1': (0.0, 0.1), 'L0_gnn_b2s': (0.0, 0.8), 'L0_gnn_b2d': (0.0, 0.8)}
    factors = {'edge_attr3_2x32': 8.0, 'L0_gnn_W2s': 8.0, 'L0_gnn_W2d': 8.0, 'L0_gnn_attn': 8.0}
    for name, (base, spread) in spreads.items():
        noise = np.random.default_rng([zlib.crc32(name.encode()), seed]).standard_normal(out[name].shape)
        drawn = base * np.exp(spread * noise) if base else spread * noise
        out[name] = jnp.asarray(drawn.astype(out[name].dtype))
    for name, factor in factors.items():
        out[name] = (out[name] * factor).astype(out[name].dtype)
    return out
```

```python
import concourse.bass as bass
from concourse import mybir
from contextlib import ExitStack


def gnn_kernel(nc, x, src, dst, edge_attr, W1, b1, W2s, b2s, W2d, b2d, attn, out):
    fp32, i32 = mybir.dt.float32, mybir.dt.int32
    ALU, ACT, AX = mybir.AluOpType, mybir.ActivationFunctionType, mybir.AxisListType
    ds = bass.ds

    N, F = x.shape
    E, H, _ = edge_attr.shape
    HF = H * F
    P = 128
    G = P // F
    EPS, SLOPE = 1e-5, 0.2

    C = -(-E // P)
    LASTROW = E - (P - 1) * C
    CC = 28
    K = C // CC
    assert C == K * CC
    NOWHERE = 2 * N
    COLS = (16, 12)
    OFF = (0, 16)
    UNITS = tuple([(c, min(2 * G, n - c)) for c in range(0, n, 2 * G)] for n in COLS)
    UPC = sum(len(u) for u in UNITS)
    BIG = 1.5e38

    PN = 125
    NN = N // PN
    PA = 112
    U = 4 * G
    MU = NN // U // K
    FIRSTN = NN - K * MU * U
    MN = MU * U
    assert FIRSTN == U and N == PN * NN

    x_n = x.rearrange("(p n) f -> p n f", p=PN)
    out_n = out.rearrange("(p n) f -> p n f", p=PN)
    r_e = edge_attr.rearrange("e h f -> e (h f)")

    ctx = ExitStack()
    with ctx:
        def sb(name, shape, dt=fp32):
            return ctx.enter_context(nc.sbuf_tensor(name, shape, dt))

        def pb(name):
            return ctx.enter_context(nc.psum_tensor(name, [P, 512], fp32))

        def sem(name):
            return ctx.enter_context(nc.semaphore(name))

        ident = sb("ident", [P, P])
        w2s_blocks = sb("w2s_blocks", [P, G * HF])
        w2d_blocks = sb("w2d_blocks", [P, G * HF])
        w1_blocks = sb("w1_blocks", [P, G * F])
        ones_row = sb("ones_row", [1, P])
        b2s_row = sb("b2s_row", [1, G * HF])
        b2d_row = sb("b2d_row", [1, G * HF])
        b2sd_row = sb("b2sd_row", [1, G * HF])
        b1_row = sb("b1_row", [1, G * F])
        attn_all = sb("attn_all", [P, HF])
        eps = sb("eps", [P, 1])
        src_idx = sb("src_idx", [P, C + CC], i32)
        dst_ext = sb("dst_ext", [P, C + 2 + CC], i32)
        dst_f = sb("dst_f", [P, C + 2])
        idx_s = [sb(f"idx_s{b}", [P, COLS[b]], i32) for b in (0, 1)]
        idx_d = [sb(f"idx_d{b}", [P, COLS[b]], i32) for b in (0, 1)]
        real = sb("real", [P, C])
        cont = sb("cont", [P, C])
        cnext = sb("cnext", [P, C])
        last = sb("last", [P, C])
        head = sb("head", [P, C])
        tail = sb("tail", [P, C])
        reset = sb("reset", [P, C])
        reset_head = sb("reset_head", [P, C])
        close = sb("close", [P, C])
        keep = sb("keep", [P, C])
        moved = sb("moved", [P, C])
        scat_idx = sb("scat_idx", [P, C], i32)
        fix_f = sb("fix_f", [P, 1])
        fix_idx = sb("fix_idx", [P, 1], i32)
        whole = sb("whole", [P, 2, F])
        whole_row = sb("whole_row", [F, 2, P])
        reset_row = sb("reset_row", [F, P])
        er = sb("er", [P, C, HF])
        base = sb("base", [P, C, F])
        score = sb("score", [P, H, C])
        xe = [sb(f"xe{b}", [P, 2, COLS[b], F]) for b in (0, 1)]
        xce = [sb(f"xce{b}", [P, 2, COLS[b], F]) for b in (0, 1)]
        sqe = [sb(f"sqe{b}", [P, 2, COLS[b], F]) for b in (0, 1)]
        leak = [sb(f"leak{b}", [P, COLS[b], HF]) for b in (0, 1)]
        sume = sb("sume", [P, 2 * COLS[0]])
        vare = sb("vare", [P, 2 * COLS[0]])
        stde = sb("stde", [P, 2 * COLS[0]])
        rstde = sb("rstde", [P, 2 * COLS[0]])
        mxe = sb("mxe", [P, H * COLS[0]])
        hte = sb("hte", [P, 4 * P])
        small_s = sb("small_s", [P, 2 * G * HF])
        xm = sb("xm", [P, MN, F])
        xcm = sb("xcm", [P, MN, F])
        sqm = sb("sqm", [P, MN, F])
        summ = sb("summ", [P, MN])
        varm = sb("varm", [P, MN])
        stdm = sb("stdm", [P, MN])
        rstdm = sb("rstdm", [P, MN])
        htm = sb("htm", [P, 4 * PN])
        fwd = sb("fwd", [P, H, C])
        full = sb("full", [P, H, C])
        prob = sb("prob", [P, H, C])
        alpha = sb("alpha", [P, H, C])
        left_max = sb("left_max", [F, P + 1])
        left_sum = sb("left_sum", [F, P + 1])
        right_row = sb("right_row", [F, P + 1])
        carry = sb("carry", [P, 4, H])
        z = [xce[b][:].rearrange("p s c f -> p (s c f)").rearrange("p (c h f) -> p c h f", h=H, f=F) for b in (0, 1)]
        cont_f = [sb(f"cont_f{b}", [P, F, COLS[b]]) for b in (0, 1)]
        msg = [sb(f"msg{b}", [P, F, COLS[b]]) for b in (0, 1)]
        run = [sb(f"run{b}", [P, F, COLS[b]]) for b in (0, 1)]
        run_t = [sb(f"run_t{b}", [P, COLS[b], F]) for b in (0, 1)]
        closed = sb("closed", [P, F * COLS[0]])
        closed_part = sb("closed_part", [P, F])
        rows = [sb(f"rows{b}", [P, COLS[b], F]) for b in (0, 1)]
        ring = [sb(f"ring{b}", [P, COLS[b]], i32) for b in (0, 1)]
        esum = sb("esum", [P, H * COLS[0]])
        rsum = sb("rsum", [P, H * COLS[0]])
        closed_sum = sb("closed_sum", [P, F])
        fix_in = sb("fix_in", [P, F])
        fix_t = sb("fix_t", [F, P])
        fix_rows = sb("fix_rows", [P, F])
        ut = hte

        ps_te = pb("ps_te")
        ps_en = pb("ps_en")
        ps_s = pb("ps_s")
        ps_b = pb("ps_b")
        ps_tm = pb("ps_tm")
        ps_om = pb("ps_om")
        ps_row = pb("ps_row")

        s_zero = sem("s_zero")
        s_idx = sem("s_idx")
        s_w = sem("s_w")
        s_attr = sem("s_attr")
        s_ident = sem("s_ident")
        s_const = sem("s_const")
        s_load = sem("s_load")
        s_store = sem("s_store")
        s_setup = sem("s_setup")
        s_b2sd = sem("s_b2sd")
        s_whole = sem("s_whole")
        s_ends = sem("s_ends")
        s_rowt = sem("s_rowt")
        s_ring = sem("s_ring")
        s_begun = sem("s_begun")
        s_gather = [sem(f"s_gather{b}") for b in (0, 1)]
        s_esum = sem("s_esum")
        s_ecent = sem("s_ecent")
        s_esq = sem("s_esq")
        s_evar = sem("s_evar")
        s_estd = sem("s_estd")
        s_erstd = sem("s_erstd")
        s_enorm = sem("s_enorm")
        s_mx = sem("s_mx")
        s_shift = sem("s_shift")
        s_watt = sem("s_watt")
        s_score = sem("s_score")
        s_te = sem("s_te")
        s_hte = sem("s_hte")
        s_en = sem("s_en")
        s_s = sem("s_s")
        s_b = sem("s_b")
        s_er = sem("s_er")
        s_base = sem("s_base")
        s_small = sem("s_small")
        s_leak = sem("s_leak")
        s_msum = sem("s_msum")
        s_mcent = sem("s_mcent")
        s_msq = sem("s_msq")
        s_mvar = sem("s_mvar")
        s_mstd = sem("s_mstd")
        s_mrstd = sem("s_mrstd")
        s_mnorm = sem("s_mnorm")
        s_tm = sem("s_tm")
        s_htm = sem("s_htm")
        s_om = sem("s_om")
        s_done = sem("s_done")
        s_less = sem("s_less")
        s_exp = sem("s_exp")
        s_z = sem("s_z")
        s_ez = sem("s_ez")
        s_zsum = sem("s_zsum")
        s_zr = sem("s_zr")
        s_zn = sem("s_zn")
        s_msg = sem("s_msg")
        s_carried = sem("s_carried")
        s_contf = sem("s_contf")
        s_run = sem("s_run")
        s_runt = sem("s_runt")
        s_cl = sem("s_cl")
        s_cls = sem("s_cls")
        s_fsum = sem("s_fsum")
        s_scidx = sem("s_scidx")
        s_scat = [sem(f"s_scat{b}") for b in (0, 1)]
        s_tu = sem("s_tu")
        s_ut = sem("s_ut")
        s_ou = sem("s_ou")
        s_row = sem("s_row")
        s_fix = sem("s_fix")
        s_fixt = sem("s_fixt")
        s_fixs = sem("s_fixs")
        s_fixed = sem("s_fixed")

        def chunks(engine, body):
            body(0)
            with engine.Fori(1, K) as k:
                body(k)

        def later(k):
            return not isinstance(k, int) or k > 0

        batches = [(b, i, c, n) for b in (0, 1) for i, (c, n) in enumerate(UNITS[b])]
        unit_no = {(b, i): q for q, (b, i, _, _) in enumerate(batches)}

        def unit_end(k, b):
            return UPC * k + unit_no[b, len(UNITS[b]) - 1] + 1

        block = ctx.enter_context(nc.Block())

        @block.sync
        def _(sp):
            sp.wait_ge(s_zero, 1)
            sp.dma_start(src_idx[0:P - 1, 0:C], src[0:(P - 1) * C].rearrange("(p c) -> p c", c=C)).then_inc(s_idx, 16)
            sp.dma_start(src_idx[P - 1:P, 0:LASTROW], src[(P - 1) * C:E].rearrange("(p c) -> p c", p=1)).then_inc(s_idx, 16)
            sp.dma_start(dst_ext[0:1, 1:C + 2], dst[0:C + 1].rearrange("(p c) -> p c", p=1)).then_inc(s_idx, 16)
            inner = bass.AP(tensor=dst.tensor, offset=dst.offset + C - 1, ap=[[C, P - 2], [1, C + 2]])
            sp.dma_start(dst_ext[1:P - 1, 0:C + 2], inner).then_inc(s_idx, 16)
            sp.dma_start(dst_ext[P - 1:P, 0:LASTROW + 1],
                         dst[(P - 1) * C - 1:E].rearrange("(p c) -> p c", p=1)).then_inc(s_idx, 16)

            def load(n0, n):
                for p0, p1 in ((0, PA), (PA, PN)):
                    sp.dma_start(xm[p0:p1, 0:n, :], x_n[p0:p1, ds(n0, n), :]).then_inc(s_load, 16)

            def store(n0, n):
                for p0, p1 in ((0, PA), (PA, PN)):
                    sp.dma_start(out_n[p0:p1, ds(n0, n), :], xm[p0:p1, 0:n, :]).then_inc(s_store, 16)

            load(0, U)
            sp.wait_ge(s_zero, 2)
            for p0, p1, c in ((0, PA, C), (PA, P - 1, C), (P - 1, P, LASTROW)):
                sp.dma_start(er[p0:p1, 0:c, :],
                             r_e[p0 * C:p0 * C + (p1 - p0 - 1) * C + c, :].rearrange("(p c) j -> p c j", c=c)
                             ).then_inc(s_attr, 16)
            sp.wait_ge(s_done, 1)
            store(0, U)

            def chunk(k):
                sp.wait_ge(s_store, 32 * (k + 1))
                load(k * MN + U, MN)
                sp.wait_ge(s_done, (k + 1) * MU + 1)
                store(k * MN + U, MN)
            with sp.Fori(0, K) as k:
                chunk(k)

        @block.gpsimd
        def _(pool):
            nc.gpsimd.memset(ident[:], 0.0).then_inc(s_ident, 1)
            pool.wait_ge(s_ident, 1)
            nc.gpsimd.affine_select(out=ident[:], in_=ident[:], compare_op=ALU.not_equal, fill=1.0, base=0,
                                    pattern=[[-1, P]], channel_multiplier=1).then_inc(s_ident, 1)

            def gather(k):
                for b in (0, 1):
                    pool.wait_ge(s_ring, 2 * k + b + 1)
                    if later(k):
                        pool.wait_ge(s_base, unit_end(k - 1, b))
                    pool.sem_inc(s_begun, 1)
                    for j in range(COLS[b]):
                        for side, idx in ((0, idx_s[b]), (1, idx_d[b])):
                            nc.gpsimd.indirect_dma_start(
                                xe[b][:, side, j, :], None, x,
                                bass.IndirectOffsetOnAxis(ap=idx[:, j:j + 1], axis=0)).then_inc(s_gather[b], 16)
            chunks(pool, gather)

            pool.wait_ge(s_store, 32 * (K + 1))

            def scatter(k):
                for b in (0, 1):
                    pool.wait_ge(s_scidx, 2 * k + b + 1)
                    pool.wait_ge(s_row, unit_end(k, b))
                    pool.sem_inc(s_begun, 1)
                    for j in range(COLS[b]):
                        nc.gpsimd.indirect_dma_start(
                            out, bass.IndirectOffsetOnAxis(ap=ring[b][:, j:j + 1], axis=0),
                            rows[b][:, j, :], None, bounds_check=N - 1, oob_is_err=False).then_inc(s_scat[b], 16)
            chunks(pool, scatter)
            pool.wait_ge(s_fixs, 1)
            nc.gpsimd.indirect_dma_start(
                out, bass.IndirectOffsetOnAxis(ap=fix_idx[:], axis=0), fix_rows[:], None,
                bounds_check=N - 1, oob_is_err=False).then_inc(s_fixed, 16)
            for b in (0, 1):
                pool.wait_ge(s_scat[b], 16 * COLS[b] * K)
            pool.wait_ge(s_fixed, 16)

        @block.scalar
        def _(act):
            act.wait_ge(s_const, 1)
            for c in range(G):
                for dest, w in ((w2s_blocks, W2s), (w2d_blocks, W2d), (w1_blocks, W1)):
                    m = w.shape[1]
                    act.dma_start(dest[c * F:(c + 1) * F, c * m:(c + 1) * m], w).then_inc(s_w, 16)
            one = lambda v: v.rearrange("(a b) -> a b", a=1)
            for dest, v in ((b2s_row, b2s), (b2d_row, b2d), (b1_row, b1)):
                m = v.shape[0]
                for c in range(G):
                    act.dma_start(dest[:, c * m:(c + 1) * m], one(v)).then_inc(s_w, 16)
            act.dma_start(attn_all[:], attn.rearrange("a h f -> a (h f)").to_broadcast([P, HF])).then_inc(s_w, 16)

            def nodes(units, t, u0):
                n = units * U
                act.wait_ge(s_mcent, t)
                nc.scalar.activation(sqm[0:PN, 0:n, :], xcm[0:PN, 0:n, :], ACT.Square).then_inc(s_msq, 1)
                act.wait_ge(s_mvar, t)
                nc.scalar.activation(stdm[0:PN, 0:n], varm[0:PN, 0:n], ACT.Sqrt, scale=1.0 / F,
                                     bias=eps[0:PN, :]).then_inc(s_mstd, 1)
                for j in range(units):
                    act.wait_ge(s_tm, u0 + j + 1)
                    if not isinstance(u0, int) or u0 + j > 0:
                        act.wait_ge(s_om, u0 + j)
                    nc.scalar.activation(htm[:], ps_tm[:, 0:4 * PN], ACT.Relu).then_inc(s_htm, 1)

            nodes(1, 1, 0)

            def chunk(k):
                for b in (0, 1):
                    t = 2 * k + b + 1
                    act.wait_ge(s_ecent, t)
                    nc.scalar.activation(sqe[b][:], xce[b][:], ACT.Square).then_inc(s_esq, 1)
                    act.wait_ge(s_evar, t)
                    nc.scalar.activation(stde[:, 0:2 * COLS[b]], vare[:, 0:2 * COLS[b]], ACT.Sqrt, scale=1.0 / F,
                                         bias=eps[:]).then_inc(s_estd, 1)
                    for i, (c, n) in enumerate(UNITS[b]):
                        q = UPC * k + unit_no[b, i]
                        act.wait_ge(s_te, q + 1)
                        if later(k) or unit_no[b, i]:
                            act.wait_ge(s_b, q)
                        nc.scalar.activation(hte[:, 0:n * 2 * F], ps_te[:, 0:n * 2 * F], ACT.Relu).then_inc(s_hte, 1)
                        act.wait_ge(s_s, q + 1)
                        if later(k) or unit_no[b, i]:
                            act.wait_ge(s_leak, q)
                        nc.scalar.activation(small_s[:, 0:n * HF], ps_s[:, 0:n * HF], ACT.Copy,
                                             scale=SLOPE).then_inc(s_small, 1)
                    if b == 0:
                        nodes(MU, k + 2, k * MU + 1)
            chunks(act, chunk)

            act.wait_ge(s_less, 1)
            nc.scalar.activation(prob[:], prob[:], ACT.Exp).then_inc(s_exp, 1)

            def third(k):
                for b in (0, 1):
                    t = 2 * k + b + 1
                    if later(k):
                        act.wait_ge(s_run, t - 2)
                    nc.scalar.activation(
                        cont_f[b][:, :, 1:COLS[b]],
                        cont[:, ds(k * CC + OFF[b] + 1, COLS[b] - 1)].rearrange("p (a c) -> p a c", a=1).to_broadcast([P, F, COLS[b] - 1]),
                        ACT.Copy).then_inc(s_contf, 1)
                    act.wait_ge(s_z, t)
                    nc.scalar.activation(z[b], z[b], ACT.Exp).then_inc(s_ez, 1)
                    act.wait_ge(s_run, t)
                    nc.scalar.activation(run_t[b][:], run[b][:].rearrange("p f c -> p c f"), ACT.Copy).then_inc(s_runt, 1)
                    for i, (c, n) in enumerate(UNITS[b]):
                        q = UPC * k + unit_no[b, i]
                        act.wait_ge(s_tu, q + 1)
                        if later(k) or unit_no[b, i]:
                            act.wait_ge(s_ou, q)
                        nc.scalar.activation(ut[:, 0:n * F], ps_te[:, 0:n * F], ACT.Copy).then_inc(s_ut, 1)
            chunks(act, third)

        @block.tensor
        def _(pe):
            pe.wait_ge(s_ident, 2)
            pe.wait_ge(s_w, 16 * (6 * G + 1))
            pe.wait_ge(s_const, 2)
            pe.wait_ge(s_b2sd, 1)

            def nodes(units, t, u0):
                pe.wait_ge(s_mnorm, t)
                for j in range(units):
                    if not isinstance(u0, int) or u0 + j > 0:
                        pe.wait_ge(s_htm, u0 + j)
                    for g in range(4):
                        a = j * U + g * G
                        m = nc.tensor.transpose(ps_tm[:, g * PN:(g + 1) * PN],
                                                xcm[0:PN, a:a + G, :].rearrange("p a f -> p (a f)"),
                                                ident[0:PN, 0:PN])
                    m.then_inc(s_tm, 1)
                    pe.wait_ge(s_htm, u0 + j + 1)
                    if not isinstance(u0, int) or u0 + j > 0:
                        pe.wait_ge(s_done, u0 + j)
                    for g in range(4):
                        o = ps_om[0:PN, g * P:(g + 1) * P]
                        nc.tensor.matmul(o, ones_row[0:1, 0:PN], b1_row[0:1, :], start=True, stop=False)
                        m = nc.tensor.matmul(o, htm[:, g * PN:(g + 1) * PN], w1_blocks[:], start=False, stop=True)
                    m.then_inc(s_om, 1)

            nodes(1, 1, 0)
            pe.wait_ge(s_whole, 2)
            for w in (0, 1):
                m = nc.tensor.transpose(ps_row[0:F, w * P:(w + 1) * P], whole[:, w, :], ident[:])
            m.then_inc(s_rowt, 1)

            def chunk(k):
                for b in (0, 1):
                    pe.wait_ge(s_enorm, 2 * k + b + 1)
                    for i, (c, n) in enumerate(UNITS[b]):
                        q = UPC * k + unit_no[b, i]
                        again = later(k) or unit_no[b, i]
                        if again:
                            pe.wait_ge(s_hte, q)
                        for g in range(n // G):
                            for side in (0, 1):
                                m = nc.tensor.transpose(ps_te[:, (2 * g + side) * P:(2 * g + side + 1) * P],
                                                        xce[b][:, side, c + g * G:c + (g + 1) * G, :].rearrange("p c f -> p (c f)"), ident[:])
                        m.then_inc(s_te, 1)
                        pe.wait_ge(s_hte, q + 1)
                        if again:
                            pe.wait_ge(s_leak, q)
                        hs = [hte[:, 2 * g * P:(2 * g + 1) * P] for g in range(n // G)]
                        hd = [hte[:, (2 * g + 1) * P:(2 * g + 2) * P] for g in range(n // G)]
                        for g in range(n // G):
                            o = ps_s[:, g * G * HF:(g + 1) * G * HF]
                            nc.tensor.matmul(o, ones_row[0:1, :], b2sd_row[0:1, :], start=True, stop=False)
                            nc.tensor.matmul(o, hs[g], w2s_blocks[:], start=False, stop=False)
                            m = nc.tensor.matmul(o, hd[g], w2d_blocks[:], start=False, stop=True)
                        m.then_inc(s_s, 1)
                        if again:
                            pe.wait_ge(s_er, q)
                        for g in range(n // G):
                            o = ps_en[:, g * G * HF:(g + 1) * G * HF]
                            nc.tensor.matmul(o, ones_row[0:1, :], b2s_row[0:1, :], start=True, stop=False)
                            m = nc.tensor.matmul(o, hs[g], w2s_blocks[:], start=False, stop=True)
                        m.then_inc(s_en, 1)
                        if again:
                            pe.wait_ge(s_base, q)
                        for g in range(n // G):
                            o = ps_b[:, g * G * F:(g + 1) * G * F]
                            nc.tensor.matmul(o, ones_row[0:1, :], b1_row[0:1, :], start=True, stop=False)
                            m = nc.tensor.matmul(o, hd[g], w1_blocks[:], start=False, stop=True)
                        m.then_inc(s_b, 1)
                    if b == 0:
                        nodes(MU, k + 2, k * MU + 1)
            chunks(pe, chunk)

            for r, left in enumerate((left_max, left_sum)):
                for i, (ends, back) in enumerate(((fwd[:, :, C - 1], left[0:H, 0:P]), (full[:, :, 0], right_row[0:H, 1:P + 1]))):
                    pe.wait_ge(s_ends, 6 * r + 3 * i + 2)
                    nc.tensor.transpose(ps_row[0:H, 0:P], ends, ident[:]).then_inc(s_rowt, 1)
                    pe.wait_ge(s_ends, 6 * r + 3 * i + 3)
                    nc.tensor.transpose(ps_row[:, P:P + H], back, ident[0:H, 0:H]).then_inc(s_rowt, 1)

            def third(k):
                for b in (0, 1):
                    pe.wait_ge(s_runt, 2 * k + b + 1)
                    for i, (c, n) in enumerate(UNITS[b]):
                        q = UPC * k + unit_no[b, i]
                        again = later(k) or unit_no[b, i]
                        if again:
                            pe.wait_ge(s_ut, q)
                        for g in range(n // G):
                            m = nc.tensor.transpose(ps_te[:, g * P:(g + 1) * P],
                                                    run_t[b][:, c + g * G:c + (g + 1) * G, :].rearrange("p c f -> p (c f)"),
                                                    ident[:])
                        m.then_inc(s_tu, 1)
                        pe.wait_ge(s_ut, q + 1)
                        if again:
                            pe.wait_ge(s_row, q)
                        for g in range(n // G):
                            m = nc.tensor.matmul(ps_b[:, g * G * F:(g + 1) * G * F], ut[:, g * P:(g + 1) * P],
                                                 w1_blocks[:], start=True, stop=True)
                        m.then_inc(s_ou, 1)
            chunks(pe, third)

            nc.tensor.transpose(ps_row[0:F, 0:P], run[1][:, :, COLS[1] - 1], ident[:]).then_inc(s_fixt, 1)
            pe.wait_ge(s_fix, 1)
            nc.tensor.transpose(ps_row[:, P:P + F], left_sum[:, 0:P], ident[0:F, 0:F]).then_inc(s_fixt, 1)
            pe.wait_ge(s_fix, 2)
            nc.tensor.transpose(ps_row[0:F, 2 * P:3 * P], fix_in[:], ident[:]).then_inc(s_fixt, 1)
            pe.wait_ge(s_fix, 3)
            nc.tensor.matmul(ps_row[:, 3 * P:3 * P + F], fix_t[:], w1_blocks[0:F, 0:F], start=True, stop=True).then_inc(s_fixt, 1)

        @block.vector
        def _(dve):
            V = nc.vector
            V.memset(src_idx[:], 0)
            V.memset(dst_ext[:], NOWHERE).then_inc(s_zero, 1)
            V.memset(w2s_blocks[:], 0.0)
            V.memset(w2d_blocks[:], 0.0)
            V.memset(w1_blocks[:], 0.0).then_inc(s_const, 1)
            V.memset(er[96:P, LASTROW:C, :], 0.0).then_inc(s_zero, 1)
            V.memset(eps[:], EPS)
            for b in (0, 1):
                V.memset(cont_f[b][:, :, 0:1], 0.0)
            V.memset(closed_sum[:], 0.0)
            V.memset(left_max[:, 0:1], -BIG)
            V.memset(left_sum[:, 0:1], 0.0)
            V.memset(right_row[:, P:P + 1], 0.0)
            V.memset(run[1][:, :, COLS[1] - 1:COLS[1]], 0.0)
            V.memset(ones_row[:], 1.0).then_inc(s_const, 1)

            def indices(k, b):
                c = k * CC + OFF[b]
                V.tensor_copy(idx_s[b][:], src_idx[:, ds(c, COLS[b])])
                V.tensor_scalar(idx_d[b][:], dst_ext[:, ds(c + 1, COLS[b])], float(N - 1), None, ALU.min).then_inc(s_ring, 1)

            dve.wait_ge(s_idx, 16 * 5)
            for b in (0, 1):
                indices(0, b)

            count = [0]

            def step(ins):
                count[0] += 1
                ins.then_inc(s_setup, 1)
                dve.wait_ge(s_setup, count[0])

            step(V.tensor_copy(dst_f[:], dst_ext[:, 0:C + 2]))
            here = dst_f[:, 1:C + 1]
            step(V.tensor_scalar(real[:], here, float(N), None, ALU.is_lt))
            step(V.tensor_tensor(cont[:], here, dst_f[:, 0:C], ALU.is_equal))
            step(V.tensor_tensor(cnext[:], here, dst_f[:, 2:C + 2], ALU.is_equal))
            step(V.tensor_tensor(cont[:], cont[:], real[:], ALU.mult))
            step(V.tensor_tensor(cnext[:], cnext[:], real[:], ALU.mult))
            step(V.tensor_scalar(last[:], cnext[:], -1.0, 1.0, ALU.mult, ALU.add))
            step(V.tensor_tensor_scan(head[:], cont[:], cont[:], 1.0, ALU.mult, ALU.mult))
            step(V.tensor_tensor_scan(tail[:, ::-1], cnext[:, ::-1], cnext[:, ::-1], 1.0, ALU.mult, ALU.mult))
            V.tensor_copy(whole[:, 0, :], head[:, C - 1:C].to_broadcast([P, F])).then_inc(s_whole, 1)
            V.tensor_copy(whole[:, 1, :], tail[:, 0:1].to_broadcast([P, F])).then_inc(s_whole, 1)
            step(V.tensor_scalar(reset[:], cont[:], -1.0, BIG, ALU.add, ALU.mult))
            step(V.tensor_scalar(reset_head[:], head[:], -1.0, BIG, ALU.add, ALU.mult))
            step(V.tensor_tensor(close[:], last[:], head[:], ALU.mult))
            step(V.tensor_tensor(keep[:], last[:], close[:], ALU.subtract))
            step(V.scalar_tensor_tensor(moved[:], here, float(NOWHERE), keep[:], ALU.subtract, ALU.mult))
            step(V.tensor_scalar(scat_idx[:], moved[:], float(NOWHERE), None, ALU.add))
            step(V.scalar_tensor_tensor(moved[:], here, float(NOWHERE), close[:], ALU.subtract, ALU.mult))
            step(V.reduce_sum(fix_f[:], moved[:], AX.X))
            step(V.tensor_scalar(fix_idx[:], fix_f[:], float(NOWHERE), None, ALU.add))

            def nodes(units, t, u0):
                n = units * U
                a, ac, sq = xm[0:PN, 0:n, :], xcm[0:PN, 0:n, :], sqm[0:PN, 0:n, :]
                over = lambda v: v[0:PN, 0:n].rearrange("p (a b) -> p a b", b=1).to_broadcast([PN, n, F])
                dve.wait_ge(s_load, 32 * t)
                V.reduce_sum(summ[0:PN, 0:n], a, AX.X).then_inc(s_msum, 1)
                dve.wait_ge(s_msum, t)
                V.scalar_tensor_tensor(ac, over(summ), -1.0 / F, a, ALU.mult, ALU.add).then_inc(s_mcent, 1)
                dve.wait_ge(s_msq, t)
                V.reduce_sum(varm[0:PN, 0:n], sq, AX.X).then_inc(s_mvar, 1)
                dve.wait_ge(s_mstd, t)
                V.reciprocal(rstdm[0:PN, 0:n], stdm[0:PN, 0:n]).then_inc(s_mrstd, 1)
                dve.wait_ge(s_mrstd, t)
                V.tensor_tensor(ac, ac, over(rstdm), ALU.mult).then_inc(s_mnorm, 1)
                for j in range(units):
                    o = xm[0:PN, j * U:(j + 1) * U, :].rearrange("p a f -> p (a f)")
                    dve.wait_ge(s_om, u0 + j + 1)
                    V.tensor_tensor(o, ps_om[0:PN, :], o, ALU.add).then_inc(s_done, 1)

            dve.wait_ge(s_w, 16 * (6 * G + 1))
            V.tensor_tensor(b2sd_row[:], b2s_row[:], b2d_row[:], ALU.add).then_inc(s_b2sd, 1)
            nodes(1, 1, 0)
            dve.wait_ge(s_rowt, 1)
            step(V.tensor_copy(whole_row[:].rearrange("f w p -> f (w p)"), ps_row[0:F, 0:2 * P]))
            step(V.tensor_scalar(reset_row[:], whole_row[:, 0, :], -1.0, BIG, ALU.add, ALU.mult))
            dve.wait_ge(s_attr, 48)

            def chunk(k):
                for b in (0, 1):
                    t = 2 * k + b + 1
                    n = COLS[b]
                    dve.wait_ge(s_gather[b], 16 * 2 * n * (k + 1))
                    indices(k + 1, b)
                    a = xe[b][:].rearrange("p s c f -> p (s c) f")
                    ac = xce[b][:].rearrange("p s c f -> p (s c) f")
                    sq = sqe[b][:].rearrange("p s c f -> p (s c) f")
                    over = lambda v: v[:, 0:2 * n].rearrange("p (a b) -> p a b", b=1).to_broadcast([P, 2 * n, F])
                    V.reduce_sum(sume[:, 0:2 * n], a, AX.X).then_inc(s_esum, 1)
                    dve.wait_ge(s_esum, t)
                    V.scalar_tensor_tensor(ac, over(sume), -1.0 / F, a, ALU.mult, ALU.add).then_inc(s_ecent, 1)
                    dve.wait_ge(s_esq, t)
                    V.reduce_sum(vare[:, 0:2 * n], sq, AX.X).then_inc(s_evar, 1)
                    dve.wait_ge(s_estd, t)
                    V.reciprocal(rstde[:, 0:2 * n], stde[:, 0:2 * n]).then_inc(s_erstd, 1)
                    dve.wait_ge(s_erstd, t)
                    V.tensor_tensor(ac, ac, over(rstde), ALU.mult).then_inc(s_enorm, 1)
                    for i, (c, m) in enumerate(UNITS[b]):
                        q = UPC * k + unit_no[b, i]
                        cols = ds(k * CC + OFF[b] + c, m)
                        flat = lambda v: v.rearrange("p c j -> p (c j)")
                        dve.wait_ge(s_small, q + 1)
                        V.tensor_tensor(flat(leak[b][:, c:c + m, :]), ps_s[:, 0:m * HF], small_s[:, 0:m * HF],
                                        ALU.max).then_inc(s_leak, 1)
                        dve.wait_ge(s_en, q + 1)
                        V.tensor_tensor(flat(er[:, cols, :]), ps_en[:, 0:m * HF], flat(er[:, cols, :]),
                                        ALU.mult).then_inc(s_er, 1)
                        dve.wait_ge(s_b, q + 1)
                        V.tensor_tensor(base[:, cols, :], ps_b[:, 0:m * F].rearrange("p (c f) -> p c f", f=F),
                                        xe[b][:, 1, c:c + m, :], ALU.add).then_inc(s_base, 1)
                    dve.wait_ge(s_base, unit_end(k, b))
                    cols = ds(k * CC + OFF[b], n)
                    rr = er[:, cols, :].rearrange("p c (h f) -> p (c h) f", h=H)
                    V.tensor_tensor(leak[b][:], leak[b][:], attn_all[:].rearrange("p (a j) -> p a j", a=1).to_broadcast([P, n, HF]),
                                    ALU.mult).then_inc(s_watt, 1)
                    dve.wait_ge(s_watt, t)
                    V.reduce_sum(score[:, :, cols].rearrange("p h c -> p c h"), leak[b][:].rearrange("p c (h f) -> p c h f", h=H),
                                 AX.X).then_inc(s_score, 1)
                    V.reduce_max(mxe[:, 0:H * n], rr, AX.X).then_inc(s_mx, 1)
                    dve.wait_ge(s_mx, t)
                    V.tensor_tensor(rr, rr, mxe[:, 0:H * n].rearrange("p (a b) -> p a b", b=1).to_broadcast([P, H * n, F]),
                                    ALU.subtract).then_inc(s_shift, 1)
                    if b == 0:
                        nodes(MU, k + 2, k * MU + 1)
            chunks(V, chunk)

            dve.wait_ge(s_score, 2 * K)
            over_heads = lambda v: v[:].rearrange("p (a c) -> p a c", a=1).to_broadcast([P, H, C])
            for r, (values, first, row_flag, op, row_op, flag, head_flag, left) in enumerate((
                    (score, -BIG, reset_row[0:H, :], ALU.add, ALU.max, reset, reset_head, left_max),
                    (prob, 0.0, whole_row[0:H, 0, :], ALU.mult, ALU.add, cont, head, left_sum))):
                for h in range(H):
                    V.tensor_tensor_scan(fwd[:, h, :], flag[:], values[:, h, :], first, op, row_op).then_inc(s_ends, 1)
                dve.wait_ge(s_rowt, 4 * r + 2)
                V.tensor_tensor_scan(left[0:H, 1:P + 1], row_flag, ps_row[0:H, 0:P], first, op, row_op).then_inc(s_ends, 1)
                dve.wait_ge(s_rowt, 4 * r + 3)
                step(V.tensor_copy(carry[:, 2 * r, :], ps_row[:, P:P + H]))
                for h in range(H):
                    step(V.scalar_tensor_tensor(fwd[:, h, :], head_flag[:], carry[:, 2 * r, h:h + 1], fwd[:, h, :], op, row_op))
                step(V.tensor_tensor(alpha[:], fwd[:], over_heads(last), ALU.mult))
                for h in range(H):
                    V.tensor_tensor_scan(full[:, h, ::-1], cnext[:, ::-1], alpha[:, h, ::-1], 0.0, ALU.mult, ALU.add).then_inc(s_ends, 1)
                dve.wait_ge(s_rowt, 4 * r + 4)
                V.tensor_tensor_scan(right_row[0:H, P - 1::-1], whole_row[0:H, 1, ::-1], ps_row[0:H, P - 1::-1], 0.0,
                                     ALU.mult, ALU.add).then_inc(s_ends, 1)
                dve.wait_ge(s_rowt, 4 * r + 5)
                step(V.tensor_copy(carry[:, 2 * r + 1, :], ps_row[:, P:P + H]))
                for h in range(H):
                    step(V.scalar_tensor_tensor(full[:, h, :], tail[:], carry[:, 2 * r + 1, h:h + 1], full[:, h, :], ALU.mult, ALU.add))
                if r == 0:
                    V.tensor_tensor(prob[:], score[:], full[:], ALU.subtract).then_inc(s_less, 1)
                    dve.wait_ge(s_exp, 1)
            step(V.tensor_scalar(full[:], full[:], 1e-9, None, ALU.max))
            step(V.reciprocal(full[:], full[:]))
            step(V.tensor_tensor(alpha[:], prob[:], full[:], ALU.mult))

            def third(k):
                for b in (0, 1):
                    t = 2 * k + b + 1
                    n, m_before = COLS[b], COLS[1 - b]
                    cols = ds(k * CC + OFF[b], n)
                    e4 = z[b]
                    e3 = z[b].rearrange("p c h f -> p (c h) f")
                    V.tensor_tensor(e4, er[:, cols, :].rearrange("p c (h f) -> p c h f", h=H),
                                    alpha[:, :, cols].rearrange("p h (c a) -> p c h a", a=1).to_broadcast([P, n, H, F]),
                                    ALU.mult).then_inc(s_z, 1)
                    dve.wait_ge(s_ez, t)
                    V.reduce_sum(esum[:, 0:H * n], e3, AX.X).then_inc(s_zsum, 1)
                    dve.wait_ge(s_zsum, t)
                    V.reciprocal(rsum[:, 0:H * n], esum[:, 0:H * n]).then_inc(s_zr, 1)
                    dve.wait_ge(s_zr, t)
                    V.tensor_tensor(e3, e3, rsum[:, 0:H * n].rearrange("p (a b) -> p a b", b=1).to_broadcast([P, H * n, F]),
                                    ALU.mult).then_inc(s_zn, 1)
                    dve.wait_ge(s_zn, t)
                    V.tensor_tensor(msg[b][:].rearrange("p f c -> p c f"), e4[:, :, 0, :], e4[:, :, 1, :],
                                    ALU.add).then_inc(s_msg, 1)
                    dve.wait_ge(s_msg, t)
                    V.scalar_tensor_tensor(msg[b][:, :, 0], run[1 - b][:, :, m_before - 1], cont[:, ds(k * CC + OFF[b], 1)],
                                           msg[b][:, :, 0], ALU.mult, ALU.add).then_inc(s_carried, 1)
                    dve.wait_ge(s_carried, t)
                    dve.wait_ge(s_contf, t)
                    V.tensor_tensor_scan(run[b][:].rearrange("p f c -> p (f c)"), cont_f[b][:].rearrange("p f c -> p (f c)"),
                                         msg[b][:].rearrange("p f c -> p (f c)"), 0.0, ALU.mult, ALU.add).then_inc(s_run, 1)
                    dve.wait_ge(s_run, t)
                    cl = closed[:, 0:F * n].rearrange("p (f c) -> p f c", c=n)
                    V.tensor_tensor(cl, run[b][:], close[:, cols].rearrange("p (a c) -> p a c", a=1).to_broadcast([P, F, n]),
                                    ALU.mult).then_inc(s_cl, 1)
                    dve.wait_ge(s_cl, t)
                    V.reduce_sum(closed_part[:], cl, AX.X).then_inc(s_cls, 1)
                    dve.wait_ge(s_cls, t)
                    V.tensor_tensor(closed_sum[:], closed_sum[:], closed_part[:], ALU.add).then_inc(s_fsum, 1)
                    if later(k):
                        dve.wait_ge(s_scat[b], 16 * n * k)
                    V.tensor_copy(ring[b][:], scat_idx[:, cols]).then_inc(s_scidx, 1)
                    for i, (c, m) in enumerate(UNITS[b]):
                        dve.wait_ge(s_ou, UPC * k + unit_no[b, i] + 1)
                        V.tensor_tensor(rows[b][:, c:c + m, :], ps_b[:, 0:m * F].rearrange("p (c f) -> p c f", f=F),
                                        base[:, ds(k * CC + OFF[b] + c, m), :], ALU.add).then_inc(s_row, 1)
            chunks(V, third)

            dve.wait_ge(s_fixt, 1)
            V.tensor_tensor_scan(left_sum[:, 1:P + 1], whole_row[:, 0, :], ps_row[0:F, 0:P], 0.0, ALU.mult, ALU.add).then_inc(s_fix, 1)
            dve.wait_ge(s_fixt, 2)
            dve.wait_ge(s_fsum, 2 * K)
            V.tensor_tensor(fix_in[:], ps_row[:, P:P + F], closed_sum[:], ALU.add).then_inc(s_fix, 1)
            dve.wait_ge(s_fixt, 3)
            V.tensor_copy(fix_t[:], ps_row[0:F, 2 * P:3 * P]).then_inc(s_fix, 1)
            dve.wait_ge(s_fixt, 4)
            V.tensor_tensor(fix_rows[:], ps_row[:, 3 * P:3 * P + F], base[:, 0, :], ALU.add).then_inc(s_fixs, 1)


_INS = ["x", "src", "dst", "edge_attr3_2x32", "L0_gnn_W1", "L0_gnn_b1", "L0_gnn_W2s", "L0_gnn_b2s",
        "L0_gnn_W2d", "L0_gnn_b2d", "L0_gnn_attn"]


def kernel(**inputs):
    import numpy as _np
    import concourse.bacc as _bacc
    from concourse import mybir as _mybir
    from concourse.bass_utils import run_bass_kernel_spmd as _run

    nc = _bacc.Bacc("TRN2", target_bir_lowering=False, num_devices=1)
    arrays, args = {}, []
    for name in _INS:
        a = _np.ascontiguousarray(inputs[name])
        arrays[f"in_{name}_dram"] = a
        args.append(nc.dram_tensor(f"in_{name}_dram", a.shape, _mybir.dt.from_np(a.dtype), kind="ExternalInput").ap())
    shape = inputs["x"].shape
    out = nc.dram_tensor("out_0_dram", shape, _mybir.dt.float32, kind="ExternalOutput").ap()
    gnn_kernel(nc, *args, out)
    r = _run(nc, [arrays], core_ids=[0])
    return r.results[0]["out_0_dram"]
```

```python
import concourse.bass as bass
from concourse import mybir
from contextlib import ExitStack


def gnn_kernel(nc, x, src, dst, edge_attr, W1, b1, W2s, b2s, W2d, b2d, attn, out):
    fp32, bf16, i32 = mybir.dt.float32, mybir.dt.bfloat16, mybir.dt.int32
    ALU, ACT, AX = mybir.AluOpType, mybir.ActivationFunctionType, mybir.AxisListType
    ds = bass.ds

    N, F = x.shape
    E, H, _ = edge_attr.shape
    HF = H * F
    P = 128
    G = P // F
    EPS, SLOPE = 1e-5, 0.2

    C = -(-E // P)
    LASTROW = E - (P - 1) * C
    CC = 28
    K = C // CC
    assert C == K * CC
    NOWHERE = 2 * N
    COLS = (16, 12)
    OFF = (0, 16)
    UNITS = tuple([(c, min(2 * G, n - c)) for c in range(0, n, 2 * G)] for n in COLS)
    UPC = sum(len(u) for u in UNITS)
    BIG = 1.5e38

    PN = 125
    NN = N // PN
    PA = 112
    U = 4 * G
    MU = NN // U // K
    FIRSTN = NN - K * MU * U
    MN = MU * U
    assert FIRSTN == U and N == PN * NN
    MS = 4
    PART = ((0, MS), (MS, MU))

    x_n = x.rearrange("(p n) f -> p n f", p=PN)
    out_n = out.rearrange("(p n) f -> p n f", p=PN)
    BIAS_STEPS = 9
    WEIGHT_DMAS = 16 * (3 * G + 4 * 3 + 1)
    r_e = edge_attr.rearrange("e h f -> e (h f)")

    ctx = ExitStack()
    with ctx:
        def sb(name, shape, dt=fp32):
            return ctx.enter_context(nc.sbuf_tensor(name, shape, dt))

        def pb(name):
            return ctx.enter_context(nc.psum_tensor(name, [P, 512], fp32))

        def sem(name):
            return ctx.enter_context(nc.semaphore(name))

        ident = sb("ident", [P, P])
        w2s_blocks = sb("w2s_blocks", [P, G * HF])
        w2d_blocks = sb("w2d_blocks", [P, G * HF])
        w1_blocks = sb("w1_blocks", [P, G * F])
        ones = sb("ones", [P, P], bf16)
        BIAS = {"b2s": (0, G * HF), "b2sd": (G * HF, 2 * G * HF), "b1": (2 * G * HF, 2 * G * HF + G * F)}
        NB = 2 * G * HF + G * F
        PARTS = (0, 32, 64)
        bias = sb("bias", [P, NB])
        bias_rest = sb("bias_rest", [P, NB])
        b2d_row = sb("b2d_row", [P, G * HF])
        bias_parts = sb("bias_parts", [P, NB], bf16)
        bias_part = sb("bias_part", [P, 3, NB], bf16)
        attn_all = sb("attn_all", [P, HF])
        eps = sb("eps", [P, 1])
        src_idx = sb("src_idx", [P, C + CC], i32)
        dst_ext = sb("dst_ext", [P, C + 2 + CC], i32)
        dst_f = sb("dst_f", [P, C + 2])
        idx_s = [sb(f"idx_s{b}", [P, COLS[b]], i32) for b in (0, 1)]
        idx_d = [sb(f"idx_d{b}", [P, COLS[b]], i32) for b in (0, 1)]
        real = sb("real", [P, C])
        cont = sb("cont", [P, C])
        cnext = sb("cnext", [P, C])
        last = sb("last", [P, C])
        head = sb("head", [P, C])
        tail = sb("tail", [P, C])
        reset = sb("reset", [P, C])
        reset_head = sb("reset_head", [P, C])
        close = sb("close", [P, C])
        keep = sb("keep", [P, C])
        moved = sb("moved", [P, C])
        scat_idx = sb("scat_idx", [P, C], i32)
        fix_f = sb("fix_f", [P, 1])
        fix_idx = sb("fix_idx", [P, 1], i32)
        whole = sb("whole", [P, 2, F])
        whole_row = sb("whole_row", [F, 2, P])
        reset_row = sb("reset_row", [F, P])
        er = sb("er", [P, C, HF])
        base = sb("base", [P, C, F])
        score = sb("score", [P, H, C])
        xe = [sb(f"xe{b}", [P, 2, COLS[b], F]) for b in (0, 1)]
        xce = [sb(f"xce{b}", [P, 2, COLS[b], F]) for b in (0, 1)]
        sqe = [sb(f"sqe{b}", [P, 2, COLS[b], F]) for b in (0, 1)]
        leak = [sb(f"leak{b}", [P, COLS[b], HF]) for b in (0, 1)]
        sume = sb("sume", [P, 2 * COLS[0]])
        vare = sb("vare", [P, 2 * COLS[0]])
        stde = sb("stde", [P, 2 * COLS[0]])
        rstde = sb("rstde", [P, 2 * COLS[0]])
        mxe = sb("mxe", [P, H * COLS[0]])
        hte = [sb(f"hte{i}", [P, 4 * P]) for i in (0, 1)]
        small_s = sb("small_s", [P, 2 * G * HF])
        xm = sb("xm", [P, MN, F])
        xcm = sb("xcm", [P, MN, F])
        sqm = sb("sqm", [P, MN, F])
        summ = sb("summ", [P, MN])
        varm = sb("varm", [P, MN])
        stdm = sb("stdm", [P, MN])
        rstdm = sb("rstdm", [P, MN])
        htm = [sb(f"htm{j}", [P, 4 * PN]) for j in (0, 1)]
        fwd = sb("fwd", [P, H, C])
        full = sb("full", [P, H, C])
        prob = sb("prob", [P, H, C])
        alpha = sb("alpha", [P, H, C])
        left_max = sb("left_max", [F, P + 1])
        left_sum = sb("left_sum", [F, P + 1])
        right_row = sb("right_row", [F, P + 1])
        carry = sb("carry", [P, 4, H])
        z = [xce[b][:].rearrange("p s c f -> p (s c f)").rearrange("p (c h f) -> p c h f", h=H, f=F) for b in (0, 1)]
        cont_f = [sb(f"cont_f{b}", [P, F, COLS[b]]) for b in (0, 1)]
        spare = xcm[:].rearrange("p a f -> p (a f)")
        taken = [0]

        def reuse(a, b):
            at = taken[0]
            taken[0] += a * b
            return spare[:, at:at + a * b].rearrange("p (a b) -> p a b", b=b)

        msg = [reuse(F, COLS[b]) for b in (0, 1)]
        run = [sb(f"run{b}", [P, F, COLS[b]]) for b in (0, 1)]
        run_t = [reuse(COLS[b], F) for b in (0, 1)]
        closed = sb("closed", [P, F * COLS[0]])
        closed_part = sb("closed_part", [P, F])
        rows = [reuse(COLS[b], F) for b in (0, 1)]
        ring = [sb(f"ring{b}", [P, COLS[b]], i32) for b in (0, 1)]
        esum = sb("esum", [P, H * COLS[0]])
        rsum = sb("rsum", [P, H * COLS[0]])
        closed_sum = sb("closed_sum", [P, F])
        fix_in = sb("fix_in", [P, F])
        fix_t = sb("fix_t", [F, P])
        fix_rows = sb("fix_rows", [P, F])
        ut = hte[0]

        ps_te = pb("ps_te")
        ps_en = pb("ps_en")
        ps_s = pb("ps_s")
        ps_b = pb("ps_b")
        ps_tm = pb("ps_tm")
        ps_om = [pb(f"ps_om{j}") for j in (0, 1)]
        ps_row = pb("ps_row")

        s_zero = sem("s_zero")
        s_idx = sem("s_idx")
        s_w = sem("s_w")
        s_attr = sem("s_attr")
        s_ident = sem("s_ident")
        s_const = sem("s_const")
        s_load = [sem(f"s_load{h}") for h in (0, 1)]
        s_store = [sem(f"s_store{h}") for h in (0, 1)]
        s_setup = sem("s_setup")
        s_bias = sem("s_bias")
        s_whole = sem("s_whole")
        s_ends = sem("s_ends")
        s_rowt = sem("s_rowt")
        s_ring = sem("s_ring")
        s_begun = sem("s_begun")
        s_gather = [sem(f"s_gather{b}") for b in (0, 1)]
        s_kept = sem("s_kept")
        s_esum = sem("s_esum")
        s_ecent = sem("s_ecent")
        s_esq = sem("s_esq")
        s_evar = sem("s_evar")
        s_estd = sem("s_estd")
        s_erstd = sem("s_erstd")
        s_enorm = sem("s_enorm")
        s_mx = sem("s_mx")
        s_shift = sem("s_shift")
        s_watt = sem("s_watt")
        s_score = sem("s_score")
        s_te = sem("s_te")
        s_hte = sem("s_hte")
        s_en = sem("s_en")
        s_s = sem("s_s")
        s_b = sem("s_b")
        s_er = sem("s_er")
        s_base = sem("s_base")
        s_small = sem("s_small")
        s_leak = sem("s_leak")
        s_msum = sem("s_msum")
        s_mcent = sem("s_mcent")
        s_msq = sem("s_msq")
        s_mvar = sem("s_mvar")
        s_mstd = sem("s_mstd")
        s_mrstd = sem("s_mrstd")
        s_mnorm = sem("s_mnorm")
        s_tm = sem("s_tm")
        s_htm = sem("s_htm")
        s_om = sem("s_om")
        s_done = sem("s_done")
        s_less = sem("s_less")
        s_exp = sem("s_exp")
        s_z = sem("s_z")
        s_ez = sem("s_ez")
        s_zsum = sem("s_zsum")
        s_zr = sem("s_zr")
        s_zn = sem("s_zn")
        s_msg = sem("s_msg")
        s_carried = sem("s_carried")
        s_contf = sem("s_contf")
        s_run = sem("s_run")
        s_runt = sem("s_runt")
        s_cl = sem("s_cl")
        s_cls = sem("s_cls")
        s_fsum = sem("s_fsum")
        s_scidx = sem("s_scidx")
        s_scat = [sem(f"s_scat{b}") for b in (0, 1)]
        s_tu = sem("s_tu")
        s_ut = sem("s_ut")
        s_ou = sem("s_ou")
        s_row = sem("s_row")
        s_fix = sem("s_fix")
        s_fixt = sem("s_fixt")
        s_fixs = sem("s_fixs")
        s_fixed = sem("s_fixed")

        def chunks(engine, body):
            body(0)
            with engine.Fori(1, K) as k:
                body(k)

        def later(k):
            return not isinstance(k, int) or k > 0

        batches = [(b, i, c, n) for b in (0, 1) for i, (c, n) in enumerate(UNITS[b])]
        unit_no = {(b, i): q for q, (b, i, _, _) in enumerate(batches)}

        def biased(which):
            c0, c1 = BIAS[which]
            return bias_parts[:, c0:c1]

        def unit_end(k, b):
            return UPC * k + unit_no[b, len(UNITS[b]) - 1] + 1

        block = ctx.enter_context(nc.Block())

        @block.sync
        def _(sp):
            sp.wait_ge(s_zero, 1)
            sp.dma_start(src_idx[0:P - 1, 0:C], src[0:(P - 1) * C].rearrange("(p c) -> p c", c=C)).then_inc(s_idx, 16)
            sp.dma_start(src_idx[P - 1:P, 0:LASTROW], src[(P - 1) * C:E].rearrange("(p c) -> p c", p=1)).then_inc(s_idx, 16)
            sp.dma_start(dst_ext[0:1, 1:C + 2], dst[0:C + 1].rearrange("(p c) -> p c", p=1)).then_inc(s_idx, 16)
            inner = bass.AP(tensor=dst.tensor, offset=dst.offset + C - 1, ap=[[C, P - 2], [1, C + 2]])
            sp.dma_start(dst_ext[1:P - 1, 0:C + 2], inner).then_inc(s_idx, 16)
            sp.dma_start(dst_ext[P - 1:P, 0:LASTROW + 1],
                         dst[(P - 1) * C - 1:E].rearrange("(p c) -> p c", p=1)).then_inc(s_idx, 16)

            def move(n0, u0, u1, out_of_x):
                for p0, p1 in ((0, PA), (PA, PN)):
                    here = xm[p0:p1, u0 * U:u1 * U, :]
                    if out_of_x:
                        sp.dma_start(here, x_n[p0:p1, ds(n0 + u0 * U, (u1 - u0) * U), :]).then_inc(s_load[u0 > 0], 16)
                    else:
                        sp.dma_start(out_n[p0:p1, ds(n0 + u0 * U, (u1 - u0) * U), :], here).then_inc(s_store[u0 > 0], 16)

            move(0, 0, 1, True)
            sp.wait_ge(s_zero, 2)
            for p0, p1, c in ((0, PA, C), (PA, P - 1, C), (P - 1, P, LASTROW)):
                sp.dma_start(er[p0:p1, 0:c, :],
                             r_e[p0 * C:p0 * C + (p1 - p0 - 1) * C + c, :].rearrange("(p c) j -> p c j", c=c)
                             ).then_inc(s_attr, 16)
            move(U, MS, MU, True)
            sp.wait_ge(s_done, 1)
            move(0, 0, 1, False)
            sp.wait_ge(s_store[0], 32)
            move(U, 0, MS, True)

            def chunk(k, more=True):
                for h, (u0, u1) in enumerate(PART):
                    sp.wait_ge(s_done, k * MU + u1 + 1)
                    move(k * MN + U, u0, u1, False)
                    if more:
                        sp.wait_ge(s_store[h], 32 * (k + 1) + 32 * (h == 0))
                        move(k * MN + MN + U, u0, u1, True)
            with sp.Fori(0, K - 1) as k:
                chunk(k)
            chunk(K - 1, more=False)

        @block.gpsimd
        def _(pool):
            nc.gpsimd.memset(ident[:], 0.0).then_inc(s_ident, 1)
            pool.wait_ge(s_ident, 1)
            nc.gpsimd.affine_select(out=ident[:], in_=ident[:], compare_op=ALU.not_equal, fill=1.0, base=0,
                                    pattern=[[-1, P]], channel_multiplier=1).then_inc(s_ident, 1)

            def gather(k):
                for b in (0, 1):
                    pool.wait_ge(s_ring, 2 * k + b + 1)
                    if later(k):
                        pool.wait_ge(s_ecent, 2 * k + b - 1)
                        pool.wait_ge(s_kept, 2 * k + b - 1)
                    pool.sem_inc(s_begun, 1)
                    for j in range(COLS[b]):
                        for side, idx in ((0, idx_s[b]), (1, idx_d[b])):
                            nc.gpsimd.indirect_dma_start(
                                xe[b][:, side, j, :], None, x,
                                bass.IndirectOffsetOnAxis(ap=idx[:, j:j + 1], axis=0)).then_inc(s_gather[b], 16)
            chunks(pool, gather)

            for h in (0, 1):
                pool.wait_ge(s_store[h], 32 * K + 32 * (h == 0))

            def scatter(k):
                for b in (0, 1):
                    pool.wait_ge(s_scidx, 2 * k + b + 1)
                    pool.wait_ge(s_row, unit_end(k, b))
                    pool.sem_inc(s_begun, 1)
                    for j in range(COLS[b]):
                        nc.gpsimd.indirect_dma_start(
                            out, bass.IndirectOffsetOnAxis(ap=ring[b][:, j:j + 1], axis=0),
                            rows[b][:, j, :], None, bounds_check=N - 1, oob_is_err=False).then_inc(s_scat[b], 16)
            chunks(pool, scatter)
            pool.wait_ge(s_fixs, 1)
            nc.gpsimd.indirect_dma_start(
                out, bass.IndirectOffsetOnAxis(ap=fix_idx[:], axis=0), fix_rows[:], None,
                bounds_check=N - 1, oob_is_err=False).then_inc(s_fixed, 16)
            for b in (0, 1):
                pool.wait_ge(s_scat[b], 16 * COLS[b] * K)
            pool.wait_ge(s_fixed, 16)

        @block.scalar
        def _(act):
            act.wait_ge(s_const, 1)
            for c in range(G):
                for dest, w in ((w2s_blocks, W2s), (w2d_blocks, W2d), (w1_blocks, W1)):
                    m = w.shape[1]
                    act.dma_start(dest[c * F:(c + 1) * F, c * m:(c + 1) * m], w).then_inc(s_w, 16)
            for p in PARTS:
                for dest, c0, v in ((bias, BIAS["b2s"][0], b2s), (bias, BIAS["b2sd"][0], b2s), (bias, BIAS["b1"][0], b1),
                                    (b2d_row, 0, b2d)):
                    m = v.shape[0]
                    act.dma_start(dest[p:p + 1, c0:c0 + G * m].rearrange("p (c m) -> p c m", m=m),
                                  v.rearrange("(a c m) -> a c m", a=1, c=1).to_broadcast([1, G, m])).then_inc(s_w, 16)
            act.dma_start(attn_all[:], attn.rearrange("a h f -> a (h f)").to_broadcast([P, HF])).then_inc(s_w, 16)

            def node_square(units, t):
                act.wait_ge(s_mcent, t)
                nc.scalar.activation(sqm[0:PN, 0:units * U, :], xcm[0:PN, 0:units * U, :], ACT.Square).then_inc(s_msq, 1)

            def node_sqrt(units, t):
                act.wait_ge(s_mvar, t)
                nc.scalar.activation(stdm[0:PN, 0:units * U], varm[0:PN, 0:units * U], ACT.Sqrt, scale=1.0 / F,
                                     bias=eps[0:PN, :]).then_inc(s_mstd, 1)

            def node_relu(units, u0):
                for j in units:
                    act.wait_ge(s_tm, u0 + j + 1)
                    if not isinstance(u0, int) or u0 + j - 1 > 0:
                        act.wait_ge(s_om, u0 + j - (j > 0))
                    nc.scalar.activation(htm[j % 2][:], ps_tm[:, 0:4 * PN], ACT.Relu).then_inc(s_htm, 1)

            def edge_relu(k, b, i):
                c, n = UNITS[b][i]
                q = UPC * k + unit_no[b, i]
                act.wait_ge(s_te, q + 1)
                if later(k) or unit_no[b, i] > 1:
                    act.wait_ge(s_b, q - 1)
                nc.scalar.activation(hte[unit_no[b, i] % 2][:, 0:n * 2 * F], ps_te[:, 0:n * 2 * F], ACT.Relu).then_inc(s_hte, 1)

            def edge_small(k, b, i):
                c, n = UNITS[b][i]
                q = UPC * k + unit_no[b, i]
                act.wait_ge(s_s, q + 1)
                if later(k) or unit_no[b, i]:
                    act.wait_ge(s_leak, q)
                nc.scalar.activation(small_s[:, 0:n * HF], ps_s[:, 0:n * HF], ACT.Copy,
                                     scale=SLOPE).then_inc(s_small, 1)

            node_square(1, 1)
            node_sqrt(1, 1)
            node_relu(range(1), 0)

            def chunk(k):
                for b in (0, 1):
                    t = 2 * k + b + 1
                    act.wait_ge(s_gather[b], 16 * 2 * COLS[b] * (k + 1))
                    nc.scalar.activation(base[:, ds(k * CC + OFF[b], COLS[b]), :], xe[b][:, 1, :, :],
                                         ACT.Copy).then_inc(s_kept, 1)
                    act.wait_ge(s_ecent, t)
                    nc.scalar.activation(sqe[b][:], xce[b][:], ACT.Square).then_inc(s_esq, 1)
                    act.wait_ge(s_evar, t)
                    nc.scalar.activation(stde[:, 0:2 * COLS[b]], vare[:, 0:2 * COLS[b]], ACT.Sqrt, scale=1.0 / F,
                                         bias=eps[:]).then_inc(s_estd, 1)
                    assert len(UNITS[b]) == 2
                    if b == 0:
                        node_square(MU, k + 2)
                    edge_relu(k, b, 0)
                    edge_relu(k, b, 1)
                    if b == 0:
                        node_sqrt(MU, k + 2)
                    edge_small(k, b, 0)
                    edge_small(k, b, 1)
                    if b == 0:
                        node_relu(range(MU), k * MU + 1)
            chunks(act, chunk)

            act.wait_ge(s_less, 1)
            nc.scalar.activation(prob[:], prob[:], ACT.Exp).then_inc(s_exp, 1)

            def third(k):
                for b in (0, 1):
                    t = 2 * k + b + 1
                    if later(k):
                        act.wait_ge(s_run, t - 2)
                    nc.scalar.activation(
                        cont_f[b][:, :, 1:COLS[b]],
                        cont[:, ds(k * CC + OFF[b] + 1, COLS[b] - 1)].rearrange("p (a c) -> p a c", a=1).to_broadcast([P, F, COLS[b] - 1]),
                        ACT.Copy).then_inc(s_contf, 1)
                    act.wait_ge(s_z, t)
                    nc.scalar.activation(z[b], z[b], ACT.Exp).then_inc(s_ez, 1)
                    act.wait_ge(s_run, t)
                    nc.scalar.activation(run_t[b], run[b][:].rearrange("p f c -> p c f"), ACT.Copy).then_inc(s_runt, 1)
                    for i, (c, n) in enumerate(UNITS[b]):
                        q = UPC * k + unit_no[b, i]
                        act.wait_ge(s_tu, q + 1)
                        if later(k) or unit_no[b, i]:
                            act.wait_ge(s_ou, q)
                        nc.scalar.activation(ut[:, 0:n * F], ps_te[:, 0:n * F], ACT.Copy).then_inc(s_ut, 1)
            chunks(act, third)

        @block.tensor
        def _(pe):
            pe.wait_ge(s_ident, 2)
            pe.wait_ge(s_w, WEIGHT_DMAS)
            pe.wait_ge(s_const, 2)
            pe.wait_ge(s_bias, BIAS_STEPS)

            def node_units(units, t, u0):
                pe.wait_ge(s_mnorm, t)

                def transposes(j):
                    if not isinstance(u0, int) or u0 + j > 0:
                        pe.wait_ge(s_htm, u0 + j)
                    for g in range(4):
                        a = j * U + g * G
                        m = nc.tensor.transpose(ps_tm[:, g * PN:(g + 1) * PN],
                                                xcm[0:PN, a:a + G, :].rearrange("p a f -> p (a f)"),
                                                ident[0:PN, 0:PN])
                    m.then_inc(s_tm, 1)

                transposes(0)
                for j in units:
                    if j + 1 < len(units):
                        transposes(j + 1)
                    if not isinstance(u0, int) or u0 + j > 1:
                        pe.wait_ge(s_done, u0 + j - 1)
                    pe.wait_ge(s_htm, u0 + j + 1)
                    for g in range(4):
                        o = ps_om[j % 2][0:PN, g * P:(g + 1) * P]
                        nc.tensor.matmul(o, ones[:, 0:PN], biased("b1"), start=True, stop=False)
                        m = nc.tensor.matmul(o, htm[j % 2][:, g * PN:(g + 1) * PN], w1_blocks[:], start=False, stop=True)
                    m.then_inc(s_om, 1)

            node_units(range(1), 1, 0)
            pe.wait_ge(s_whole, 2)
            for w in (0, 1):
                m = nc.tensor.transpose(ps_row[0:F, w * P:(w + 1) * P], whole[:, w, :], ident[:])
            m.then_inc(s_rowt, 1)

            def edge_transposes(k, b, i):
                c, n = UNITS[b][i]
                q = UPC * k + unit_no[b, i]
                if later(k) or unit_no[b, i]:
                    pe.wait_ge(s_hte, q)
                for g in range(n // G):
                    for side in (0, 1):
                        m = nc.tensor.transpose(ps_te[:, (2 * g + side) * P:(2 * g + side + 1) * P],
                                                xce[b][:, side, c + g * G:c + (g + 1) * G, :].rearrange("p c f -> p (c f)"), ident[:])
                m.then_inc(s_te, 1)

            def chunk(k):
                for b in (0, 1):
                    pe.wait_ge(s_enorm, 2 * k + b + 1)
                    edge_transposes(k, b, 0)
                    for i, (c, n) in enumerate(UNITS[b]):
                        q = UPC * k + unit_no[b, i]
                        again = later(k) or unit_no[b, i]
                        if i + 1 < len(UNITS[b]):
                            edge_transposes(k, b, i + 1)
                        pe.wait_ge(s_hte, q + 1)
                        if again:
                            pe.wait_ge(s_leak, q)
                        ht = hte[unit_no[b, i] % 2]
                        hs = [ht[:, 2 * g * P:(2 * g + 1) * P] for g in range(n // G)]
                        hd = [ht[:, (2 * g + 1) * P:(2 * g + 2) * P] for g in range(n // G)]

                        def products(ps, m, which, factors):
                            for g in range(n // G):
                                o = ps[:, g * G * m:(g + 1) * G * m]
                                nc.tensor.matmul(o, ones[:], biased(which), start=True, stop=False)
                                for f, (rows_t, w) in enumerate(factors):
                                    last_mm = nc.tensor.matmul(o, rows_t[g], w[:], start=False, stop=f == len(factors) - 1)
                            return last_mm

                        products(ps_s, HF, "b2sd", ((hs, w2s_blocks), (hd, w2d_blocks))).then_inc(s_s, 1)
                        if again:
                            pe.wait_ge(s_er, q)
                        products(ps_en, HF, "b2s", ((hs, w2s_blocks),)).then_inc(s_en, 1)
                        if again:
                            pe.wait_ge(s_base, q)
                        products(ps_b, F, "b1", ((hd, w1_blocks),)).then_inc(s_b, 1)
                    if b == 0:
                        node_units(range(MU), k + 2, k * MU + 1)
            chunks(pe, chunk)

            for r, left in enumerate((left_max, left_sum)):
                for i, (ends, back) in enumerate(((fwd[:, :, C - 1], left[0:H, 0:P]), (full[:, :, 0], right_row[0:H, 1:P + 1]))):
                    pe.wait_ge(s_ends, 6 * r + 3 * i + 2)
                    nc.tensor.transpose(ps_row[0:H, 0:P], ends, ident[:]).then_inc(s_rowt, 1)
                    pe.wait_ge(s_ends, 6 * r + 3 * i + 3)
                    nc.tensor.transpose(ps_row[:, P:P + H], back, ident[0:H, 0:H]).then_inc(s_rowt, 1)

            def third(k):
                for b in (0, 1):
                    pe.wait_ge(s_runt, 2 * k + b + 1)
                    for i, (c, n) in enumerate(UNITS[b]):
                        q = UPC * k + unit_no[b, i]
                        again = later(k) or unit_no[b, i]
                        if again:
                            pe.wait_ge(s_ut, q)
                        for g in range(n // G):
                            m = nc.tensor.transpose(ps_te[:, g * P:(g + 1) * P],
                                                    run_t[b][:, c + g * G:c + (g + 1) * G, :].rearrange("p c f -> p (c f)"),
                                                    ident[:])
                        m.then_inc(s_tu, 1)
                        pe.wait_ge(s_ut, q + 1)
                        if again:
                            pe.wait_ge(s_row, q)
                        for g in range(n // G):
                            m = nc.tensor.matmul(ps_b[:, g * G * F:(g + 1) * G * F], ut[:, g * P:(g + 1) * P],
                                                 w1_blocks[:], start=True, stop=True)
                        m.then_inc(s_ou, 1)
            chunks(pe, third)

            nc.tensor.transpose(ps_row[0:F, 0:P], run[1][:, :, COLS[1] - 1], ident[:]).then_inc(s_fixt, 1)
            pe.wait_ge(s_fix, 1)
            nc.tensor.transpose(ps_row[:, P:P + F], left_sum[:, 0:P], ident[0:F, 0:F]).then_inc(s_fixt, 1)
            pe.wait_ge(s_fix, 2)
            nc.tensor.transpose(ps_row[0:F, 2 * P:3 * P], fix_in[:], ident[:]).then_inc(s_fixt, 1)
            pe.wait_ge(s_fix, 3)
            nc.tensor.matmul(ps_row[:, 3 * P:3 * P + F], fix_t[:], w1_blocks[0:F, 0:F], start=True, stop=True).then_inc(s_fixt, 1)

        @block.vector
        def _(dve):
            V = nc.vector
            V.memset(src_idx[:], 0)
            V.memset(dst_ext[:], NOWHERE).then_inc(s_zero, 1)
            V.memset(bias[:], 0.0)
            V.memset(b2d_row[:], 0.0)
            V.memset(bias_parts[:], 0.0)
            V.memset(w2s_blocks[:], 0.0)
            V.memset(w2d_blocks[:], 0.0)
            V.memset(w1_blocks[:], 0.0).then_inc(s_const, 1)
            V.memset(er[96:P, LASTROW:C, :], 0.0).then_inc(s_zero, 1)
            V.memset(eps[:], EPS)
            for b in (0, 1):
                V.memset(cont_f[b][:, :, 0:1], 0.0)
            V.memset(closed_sum[:], 0.0)
            V.memset(left_max[:, 0:1], -BIG)
            V.memset(left_sum[:, 0:1], 0.0)
            V.memset(right_row[:, P:P + 1], 0.0)
            V.memset(run[1][:, :, COLS[1] - 1:COLS[1]], 0.0)
            V.memset(ones[:], 1.0).then_inc(s_const, 1)

            def indices(k, b):
                c = k * CC + OFF[b]
                V.tensor_copy(idx_s[b][:], src_idx[:, ds(c, COLS[b])])
                V.tensor_scalar(idx_d[b][:], dst_ext[:, ds(c + 1, COLS[b])], float(N - 1), None, ALU.min).then_inc(s_ring, 1)

            dve.wait_ge(s_idx, 16 * 5)
            for b in (0, 1):
                indices(0, b)

            count = [0]

            def step(ins):
                count[0] += 1
                ins.then_inc(s_setup, 1)
                dve.wait_ge(s_setup, count[0])

            step(V.tensor_copy(dst_f[:], dst_ext[:, 0:C + 2]))
            here = dst_f[:, 1:C + 1]
            step(V.tensor_scalar(real[:], here, float(N), None, ALU.is_lt))
            step(V.tensor_tensor(cont[:], here, dst_f[:, 0:C], ALU.is_equal))
            step(V.tensor_tensor(cnext[:], here, dst_f[:, 2:C + 2], ALU.is_equal))
            step(V.tensor_tensor(cont[:], cont[:], real[:], ALU.mult))
            step(V.tensor_tensor(cnext[:], cnext[:], real[:], ALU.mult))
            step(V.tensor_scalar(last[:], cnext[:], -1.0, 1.0, ALU.mult, ALU.add))
            step(V.tensor_tensor_scan(head[:], cont[:], cont[:], 1.0, ALU.mult, ALU.mult))
            step(V.tensor_tensor_scan(tail[:, ::-1], cnext[:, ::-1], cnext[:, ::-1], 1.0, ALU.mult, ALU.mult))
            V.tensor_copy(whole[:, 0, :], head[:, C - 1:C].to_broadcast([P, F])).then_inc(s_whole, 1)
            V.tensor_copy(whole[:, 1, :], tail[:, 0:1].to_broadcast([P, F])).then_inc(s_whole, 1)
            step(V.tensor_scalar(reset[:], cont[:], -1.0, BIG, ALU.add, ALU.mult))
            step(V.tensor_scalar(reset_head[:], head[:], -1.0, BIG, ALU.add, ALU.mult))
            step(V.tensor_tensor(close[:], last[:], head[:], ALU.mult))
            step(V.tensor_tensor(keep[:], last[:], close[:], ALU.subtract))
            step(V.scalar_tensor_tensor(moved[:], here, float(NOWHERE), keep[:], ALU.subtract, ALU.mult))
            step(V.tensor_scalar(scat_idx[:], moved[:], float(NOWHERE), None, ALU.add))
            step(V.scalar_tensor_tensor(moved[:], here, float(NOWHERE), close[:], ALU.subtract, ALU.mult))
            step(V.reduce_sum(fix_f[:], moved[:], AX.X))
            step(V.tensor_scalar(fix_idx[:], fix_f[:], float(NOWHERE), None, ALU.add))

            def over(v, p, n):
                return v[0:p, 0:n].rearrange("p (a b) -> p a b", b=1).to_broadcast([p, n, F])

            def node_norm(units, t):
                n = units * U
                a, ac, sq = xm[0:PN, 0:n, :], xcm[0:PN, 0:n, :], sqm[0:PN, 0:n, :]
                dve.wait_ge(s_load[0], 32 * t)
                if units > 1:
                    dve.wait_ge(s_load[1], 32 * (t - 1))
                V.reduce_sum(summ[0:PN, 0:n], a, AX.X).then_inc(s_msum, 1)
                yield
                dve.wait_ge(s_msum, t)
                V.scalar_tensor_tensor(ac, over(summ, PN, n), -1.0 / F, a, ALU.mult, ALU.add).then_inc(s_mcent, 1)
                yield
                dve.wait_ge(s_msq, t)
                V.reduce_sum(varm[0:PN, 0:n], sq, AX.X).then_inc(s_mvar, 1)
                yield
                dve.wait_ge(s_mstd, t)
                V.reciprocal(rstdm[0:PN, 0:n], stdm[0:PN, 0:n]).then_inc(s_mrstd, 1)
                dve.wait_ge(s_mrstd, t)
                V.tensor_tensor(ac, ac, over(rstdm, PN, n), ALU.mult).then_inc(s_mnorm, 1)
                yield

            def node_add(j, u0):
                o = xm[0:PN, j * U:(j + 1) * U, :].rearrange("p a f -> p (a f)")
                dve.wait_ge(s_om, u0 + j + 1)
                V.tensor_tensor(o, ps_om[j % 2][0:PN, :], o, ALU.add).then_inc(s_done, 1)

            dve.wait_ge(s_w, WEIGHT_DMAS)
            steps = [0]

            def split(ins):
                steps[0] += 1
                ins.then_inc(s_bias, 1)
                dve.wait_ge(s_bias, steps[0])

            c0, c1 = BIAS["b2sd"]
            split(V.tensor_tensor(bias[:, c0:c1], bias[:, c0:c1], b2d_row[:], ALU.add))
            for i, of in ((0, bias), (1, bias_rest), (2, bias_rest)):
                split(V.tensor_copy(bias_part[:, i, :], of[:]))
                if i < 2:
                    split(V.tensor_tensor(bias_rest[:], of[:], bias_part[:, i, :], ALU.subtract))
            for i, p in enumerate(PARTS):
                split(V.tensor_copy(bias_parts[p:p + 1, :], bias_part[p:p + 1, i, :]))
            assert steps[0] == BIAS_STEPS
            for _ in node_norm(1, 1):
                pass
            node_add(0, 0)
            dve.wait_ge(s_rowt, 1)
            step(V.tensor_copy(whole_row[:].rearrange("f w p -> f (w p)"), ps_row[0:F, 0:2 * P]))
            step(V.tensor_scalar(reset_row[:], whole_row[:, 0, :], -1.0, BIG, ALU.add, ALU.mult))
            dve.wait_ge(s_attr, 48)

            def edge_norm(k, b):
                t, n = 2 * k + b + 1, COLS[b]
                a = xe[b][:].rearrange("p s c f -> p (s c) f")
                ac = xce[b][:].rearrange("p s c f -> p (s c) f")
                sq = sqe[b][:].rearrange("p s c f -> p (s c) f")
                dve.wait_ge(s_gather[b], 16 * 2 * n * (k + 1))
                indices(k + 1, b)
                V.reduce_sum(sume[:, 0:2 * n], a, AX.X).then_inc(s_esum, 1)
                dve.wait_ge(s_esum, t)
                V.scalar_tensor_tensor(ac, over(sume, P, 2 * n), -1.0 / F, a, ALU.mult, ALU.add).then_inc(s_ecent, 1)
                yield
                dve.wait_ge(s_esq, t)
                V.reduce_sum(vare[:, 0:2 * n], sq, AX.X).then_inc(s_evar, 1)
                yield
                dve.wait_ge(s_estd, t)
                V.reciprocal(rstde[:, 0:2 * n], stde[:, 0:2 * n]).then_inc(s_erstd, 1)
                dve.wait_ge(s_erstd, t)
                V.tensor_tensor(ac, ac, over(rstde, P, 2 * n), ALU.mult).then_inc(s_enorm, 1)
                yield

            def edge_unit(k, b, i):
                c, m = UNITS[b][i]
                q = UPC * k + unit_no[b, i]
                cols = ds(k * CC + OFF[b] + c, m)
                flat = lambda v: v.rearrange("p c j -> p (c j)")
                dve.wait_ge(s_small, q + 1)
                V.tensor_tensor(flat(leak[b][:, c:c + m, :]), ps_s[:, 0:m * HF], small_s[:, 0:m * HF],
                                ALU.max).then_inc(s_leak, 1)
                dve.wait_ge(s_en, q + 1)
                V.tensor_tensor(flat(er[:, cols, :]), ps_en[:, 0:m * HF], flat(er[:, cols, :]),
                                ALU.mult).then_inc(s_er, 1)
                dve.wait_ge(s_b, q + 1)
                dve.wait_ge(s_kept, 2 * k + b + 1)
                V.tensor_tensor(flat(base[:, cols, :]), ps_b[:, 0:m * F], flat(base[:, cols, :]), ALU.add).then_inc(s_base, 1)

            def edge_score(k, b):
                t, n = 2 * k + b + 1, COLS[b]
                cols = ds(k * CC + OFF[b], n)
                rr = er[:, cols, :].rearrange("p c (h f) -> p (c h) f", h=H)
                dve.wait_ge(s_base, unit_end(k, b))
                V.tensor_tensor(leak[b][:], leak[b][:], attn_all[:].rearrange("p (a j) -> p a j", a=1).to_broadcast([P, n, HF]),
                                ALU.mult).then_inc(s_watt, 1)
                V.reduce_max(mxe[:, 0:H * n], rr, AX.X).then_inc(s_mx, 1)
                dve.wait_ge(s_watt, t)
                V.reduce_sum(score[:, :, cols].rearrange("p h c -> p c h"), leak[b][:].rearrange("p c (h f) -> p c h f", h=H),
                             AX.X).then_inc(s_score, 1)
                dve.wait_ge(s_mx, t)
                V.tensor_tensor(rr, rr, over(mxe, P, H * n), ALU.subtract).then_inc(s_shift, 1)

            def chunk(k):
                u0 = k * MU + 1
                edges, nodes = edge_norm(k, 0), node_norm(MU, k + 2)
                next(edges)
                next(nodes)
                next(edges)
                next(nodes)
                next(edges)
                next(nodes)
                next(nodes)
                edge_unit(k, 0, 0)
                edge_unit(k, 0, 1)
                edge_score(k, 0)
                for j in range(MS):
                    node_add(j, u0)
                edges = edge_norm(k, 1)
                next(edges)
                for j in range(MS, MU - 1):
                    node_add(j, u0)
                next(edges)
                node_add(MU - 1, u0)
                next(edges)
                for i in range(len(UNITS[1])):
                    edge_unit(k, 1, i)
                edge_score(k, 1)
            chunks(V, chunk)

            dve.wait_ge(s_score, 2 * K)
            over_heads = lambda v: v[:].rearrange("p (a c) -> p a c", a=1).to_broadcast([P, H, C])
            for r, (values, first, row_flag, op, row_op, flag, head_flag, left) in enumerate((
                    (score, -BIG, reset_row[0:H, :], ALU.add, ALU.max, reset, reset_head, left_max),
                    (prob, 0.0, whole_row[0:H, 0, :], ALU.mult, ALU.add, cont, head, left_sum))):
                for h in range(H):
                    V.tensor_tensor_scan(fwd[:, h, :], flag[:], values[:, h, :], first, op, row_op).then_inc(s_ends, 1)
                dve.wait_ge(s_rowt, 4 * r + 2)
                V.tensor_tensor_scan(left[0:H, 1:P + 1], row_flag, ps_row[0:H, 0:P], first, op, row_op).then_inc(s_ends, 1)
                dve.wait_ge(s_rowt, 4 * r + 3)
                step(V.tensor_copy(carry[:, 2 * r, :], ps_row[:, P:P + H]))
                for h in range(H):
                    step(V.scalar_tensor_tensor(fwd[:, h, :], head_flag[:], carry[:, 2 * r, h:h + 1], fwd[:, h, :], op, row_op))
                step(V.tensor_tensor(alpha[:], fwd[:], over_heads(last), ALU.mult))
                for h in range(H):
                    V.tensor_tensor_scan(full[:, h, ::-1], cnext[:, ::-1], alpha[:, h, ::-1], 0.0, ALU.mult, ALU.add).then_inc(s_ends, 1)
                dve.wait_ge(s_rowt, 4 * r + 4)
                V.tensor_tensor_scan(right_row[0:H, P - 1::-1], whole_row[0:H, 1, ::-1], ps_row[0:H, P - 1::-1], 0.0,
                                     ALU.mult, ALU.add).then_inc(s_ends, 1)
                dve.wait_ge(s_rowt, 4 * r + 5)
                step(V.tensor_copy(carry[:, 2 * r + 1, :], ps_row[:, P:P + H]))
                for h in range(H):
                    step(V.scalar_tensor_tensor(full[:, h, :], tail[:], carry[:, 2 * r + 1, h:h + 1], full[:, h, :], ALU.mult, ALU.add))
                if r == 0:
                    V.tensor_tensor(prob[:], score[:], full[:], ALU.subtract).then_inc(s_less, 1)
                    dve.wait_ge(s_exp, 1)
            step(V.tensor_scalar(full[:], full[:], 1e-9, None, ALU.max))
            step(V.reciprocal(full[:], full[:]))
            step(V.tensor_tensor(alpha[:], prob[:], full[:], ALU.mult))

            def third(k):
                for b in (0, 1):
                    t = 2 * k + b + 1
                    n, m_before = COLS[b], COLS[1 - b]
                    cols = ds(k * CC + OFF[b], n)
                    e4 = z[b]
                    e3 = z[b].rearrange("p c h f -> p (c h) f")
                    V.tensor_tensor(e4, er[:, cols, :].rearrange("p c (h f) -> p c h f", h=H),
                                    alpha[:, :, cols].rearrange("p h (c a) -> p c h a", a=1).to_broadcast([P, n, H, F]),
                                    ALU.mult).then_inc(s_z, 1)
                    dve.wait_ge(s_ez, t)
                    V.reduce_sum(esum[:, 0:H * n], e3, AX.X).then_inc(s_zsum, 1)
                    dve.wait_ge(s_zsum, t)
                    V.reciprocal(rsum[:, 0:H * n], esum[:, 0:H * n]).then_inc(s_zr, 1)
                    dve.wait_ge(s_zr, t)
                    V.tensor_tensor(e3, e3, rsum[:, 0:H * n].rearrange("p (a b) -> p a b", b=1).to_broadcast([P, H * n, F]),
                                    ALU.mult).then_inc(s_zn, 1)
                    dve.wait_ge(s_zn, t)
                    V.tensor_tensor(msg[b].rearrange("p f c -> p c f"), e4[:, :, 0, :], e4[:, :, 1, :],
                                    ALU.add).then_inc(s_msg, 1)
                    dve.wait_ge(s_msg, t)
                    V.scalar_tensor_tensor(msg[b][:, :, 0], run[1 - b][:, :, m_before - 1], cont[:, ds(k * CC + OFF[b], 1)],
                                           msg[b][:, :, 0], ALU.mult, ALU.add).then_inc(s_carried, 1)
                    dve.wait_ge(s_carried, t)
                    dve.wait_ge(s_contf, t)
                    V.tensor_tensor_scan(run[b][:].rearrange("p f c -> p (f c)"), cont_f[b][:].rearrange("p f c -> p (f c)"),
                                         msg[b].rearrange("p f c -> p (f c)"), 0.0, ALU.mult, ALU.add).then_inc(s_run, 1)
                    dve.wait_ge(s_run, t)
                    cl = closed[:, 0:F * n].rearrange("p (f c) -> p f c", c=n)
                    V.tensor_tensor(cl, run[b][:], close[:, cols].rearrange("p (a c) -> p a c", a=1).to_broadcast([P, F, n]),
                                    ALU.mult).then_inc(s_cl, 1)
                    dve.wait_ge(s_cl, t)
                    V.reduce_sum(closed_part[:], cl, AX.X).then_inc(s_cls, 1)
                    dve.wait_ge(s_cls, t)
                    V.tensor_tensor(closed_sum[:], closed_sum[:], closed_part[:], ALU.add).then_inc(s_fsum, 1)
                    if later(k):
                        dve.wait_ge(s_scat[b], 16 * n * k)
                    V.tensor_copy(ring[b][:], scat_idx[:, cols]).then_inc(s_scidx, 1)
                    for i, (c, m) in enumerate(UNITS[b]):
                        dve.wait_ge(s_ou, UPC * k + unit_no[b, i] + 1)
                        V.tensor_tensor(rows[b][:, c:c + m, :], ps_b[:, 0:m * F].rearrange("p (c f) -> p c f", f=F),
                                        base[:, ds(k * CC + OFF[b] + c, m), :], ALU.add).then_inc(s_row, 1)
            chunks(V, third)

            dve.wait_ge(s_fixt, 1)
            V.tensor_tensor_scan(left_sum[:, 1:P + 1], whole_row[:, 0, :], ps_row[0:F, 0:P], 0.0, ALU.mult, ALU.add).then_inc(s_fix, 1)
            dve.wait_ge(s_fixt, 2)
            dve.wait_ge(s_fsum, 2 * K)
            V.tensor_tensor(fix_in[:], ps_row[:, P:P + F], closed_sum[:], ALU.add).then_inc(s_fix, 1)
            dve.wait_ge(s_fixt, 3)
            V.tensor_copy(fix_t[:], ps_row[0:F, 2 * P:3 * P]).then_inc(s_fix, 1)
            dve.wait_ge(s_fixt, 4)
            V.tensor_tensor(fix_rows[:], ps_row[:, 3 * P:3 * P + F], base[:, 0, :], ALU.add).then_inc(s_fixs, 1)


_INS = ["x", "src", "dst", "edge_attr3_2x32", "L0_gnn_W1", "L0_gnn_b1", "L0_gnn_W2s", "L0_gnn_b2s",
        "L0_gnn_W2d", "L0_gnn_b2d", "L0_gnn_attn"]


def kernel(**inputs):
    import numpy as _np
    import concourse.bacc as _bacc
    from concourse import mybir as _mybir
    from concourse.bass_utils import run_bass_kernel_spmd as _run

    nc = _bacc.Bacc("TRN2", target_bir_lowering=False, num_devices=1)
    arrays, args = {}, []
    for name in _INS:
        a = _np.ascontiguousarray(inputs[name])
        arrays[f"in_{name}_dram"] = a
        args.append(nc.dram_tensor(f"in_{name}_dram", a.shape, _mybir.dt.from_np(a.dtype), kind="ExternalInput").ap())
    shape = inputs["x"].shape
    out = nc.dram_tensor("out_0_dram", shape, _mybir.dt.float32, kind="ExternalOutput").ap()
    gnn_kernel(nc, *args, out)
    r = _run(nc, [arrays], core_ids=[0])
    return r.results[0]["out_0_dram"]
```

```python
import concourse.bass as bass
from concourse import mybir
from contextlib import ExitStack


def gnn_kernel(nc, x, src, dst, edge_attr, W1, b1, W2s, b2s, W2d, b2d, attn, out):
    fp32, bf16, i32 = mybir.dt.float32, mybir.dt.bfloat16, mybir.dt.int32
    ALU, ACT, AX = mybir.AluOpType, mybir.ActivationFunctionType, mybir.AxisListType
    ds = bass.ds

    N, F = x.shape
    E, H, _ = edge_attr.shape
    HF = H * F
    P = 128
    G = P // F
    EPS, SLOPE = 1e-5, 0.2

    C = -(-E // P)
    LASTROW = E - (P - 1) * C
    CC = 28
    K = C // CC
    assert C == K * CC
    NOWHERE = 2 * N
    COLS = (16, 12)
    OFF = (0, 16)
    UNITS = tuple([(c, min(2 * G, n - c)) for c in range(0, n, 2 * G)] for n in COLS)
    UPC = sum(len(u) for u in UNITS)
    BIG = 1.5e38
    WARM_UPS = 22
    PIECE = 2500
    PIECES = E // PIECE
    KEY = 1 << 15
    assert PIECES * PIECE == E and P * C < KEY

    PN = 125
    NN = N // PN
    PA = 112
    U = 4 * G
    MU = NN // U // K
    MU0 = NN // U - (K - 1) * MU
    MN, MN0 = MU * U, MU0 * U
    assert NN == MN0 + (K - 1) * MN and MU <= MU0 and N == PN * NN
    MS = 4

    x_n = x.rearrange("(p n) f -> p n f", p=PN)
    out_n = out.rearrange("(p n) f -> p n f", p=PN)
    BIAS_STEPS = 9
    WEIGHT_DMAS = 16 * 7
    r_e = edge_attr.rearrange("e h f -> e (h f)")

    ctx = ExitStack()
    with ctx:
        def sb(name, shape, dt=fp32):
            return ctx.enter_context(nc.sbuf_tensor(name, shape, dt))

        def pb(name):
            return ctx.enter_context(nc.psum_tensor(name, [P, 512], fp32))

        def sem(name):
            return ctx.enter_context(nc.semaphore(name))

        ident = sb("ident", [P, P])
        w2s_blocks = sb("w2s_blocks", [P, G * HF])
        w2d_blocks = sb("w2d_blocks", [P, G * HF])
        w1_blocks = sb("w1_blocks", [P, G * F])
        w_all = [sb(f"w_all{i}", [P, w.shape[1]]) for i, w in enumerate((W2s, W2d, W1))]
        ones = sb("ones", [P, P], bf16)
        BIAS = {"b2s": (0, G * HF), "b2sd": (G * HF, 2 * G * HF), "b1": (2 * G * HF, 2 * G * HF + G * F)}
        NB = 2 * G * HF + G * F
        PARTS = (0, 32, 64)
        bias = sb("bias", [P, NB])
        bias_rest = sb("bias_rest", [P, NB])
        b2d_row = sb("b2d_row", [P, G * HF])
        bias_parts = sb("bias_parts", [P, NB], bf16)
        bias_part = sb("bias_part", [P, 3, NB], bf16)
        attn_all = sb("attn_all", [P, HF])
        eps = sb("eps", [P, 1])
        zeros = sb("zeros", [P, HF])
        src_idx = sb("src_idx", [P, C], i32)
        dst_ext = sb("dst_ext", [P, C + 2], i32)
        dst_f = sb("dst_f", [P, C + 2])
        idx_s = [sb(f"idx_s{b}", [P, COLS[b]], i32) for b in (0, 1)]
        idx_d = [sb(f"idx_d{b}", [P, COLS[b]], i32) for b in (0, 1)]
        cont = sb("cont", [P, C])
        cnext = sb("cnext", [P, C])
        last = sb("last", [P, C])
        head = sb("head", [P, C])
        tail = sb("tail", [P, C])
        reset = sb("reset", [P, C])
        reset_next = sb("reset_next", [P, C])
        reset_head = sb("reset_head", [P, C])
        reset_tail = sb("reset_tail", [P, C])
        close = sb("close", [P, C])
        scat_idx = sb("scat_idx", [P, C], i32)
        fix_f = sb("fix_f", [P, 1])
        fix_idx = sb("fix_idx", [P, 1], i32)
        whole = sb("whole", [P, 2, F])
        whole_row = sb("whole_row", [F, 2, P])
        reset_row = sb("reset_row", [F, 2, P])
        downs = sb("downs", [P, 1])
        ones_col = sb("ones_col", [P, 1])
        unsorted = sb("unsorted", [1, 1], i32)
        er = sb("er", [P, C, HF])
        base = sb("base", [P, C, F])
        score = sb("score", [P, H, C])
        xe = [sb(f"xe{b}", [P, 2, COLS[b], F]) for b in (0, 1)]
        xce = [sb(f"xce{b}", [P, 2, COLS[b], F]) for b in (0, 1)]
        sqe = [sb(f"sqe{b}", [P, 2, COLS[b], F]) for b in (0, 1)]
        leak = [sb(f"leak{b}", [P, COLS[b], HF]) for b in (0, 1)]
        sume = sb("sume", [P, 2 * COLS[0]])
        vare = sb("vare", [P, 2 * COLS[0]])
        stde = sb("stde", [P, 2 * COLS[0]])
        rstde = sb("rstde", [P, 2 * COLS[0]])
        mxe = sb("mxe", [P, H * COLS[0]])
        hte = [sb(f"hte{i}", [P, 4 * P]) for i in (0, 1)]
        small_s = sb("small_s", [P, 2 * G * HF])
        xm = sb("xm", [P, MN0, F])
        xcm = sb("xcm", [P, MN0, F])
        sqm = sb("sqm", [P, MN0, F])
        summ = sb("summ", [P, MN0])
        varm = sb("varm", [P, MN0])
        stdm = sb("stdm", [P, MN0])
        rstdm = sb("rstdm", [P, MN0])
        htm = [sb(f"htm{j}", [P, 4 * PN]) for j in (0, 1)]
        fwd = sb("fwd", [P, H, C])
        full = sb("full", [P, H, C])
        prob = sb("prob", [P, H, C])
        bwd = sb("bwd", [P, H, C])
        alpha = [sb(f"alpha{b}", [P, H, COLS[b]]) for b in (0, 1)]
        left_max = sb("left_max", [F, P + 1])
        left_sum = sb("left_sum", [F, P + 1])
        right_max = sb("right_max", [F, P + 1])
        right_sum = sb("right_sum", [F, P + 1])
        carry = [sb(f"carry{r}", [P, 2, H]) for r in (0, 1)]
        flat2 = lambda v: v[:].rearrange("p a b -> p (a b)")
        down, real, keep, moved = (flat2(sqm)[:, i * C:(i + 1) * C] for i in range(4))
        others = flat2(base)[:, 0:PIECE].bitcast(i32)
        others_key = flat2(base)[:, PIECE:2 * PIECE]
        others_no = flat2(sqm)[:, MN0 * F - PIECE:]
        differ = flat2(xcm)[:, MN0 * F - PIECE:]
        own_key, own_no = score[:, 0, :], score[:, 1, :]
        smaller, place = fwd[:, 0, :], fwd[:, 1, :]
        iota_i = flat2(prob)[:, 0:C].bitcast(i32)
        iota_o = flat2(xcm)[:, MN0 * F - PIECE:].bitcast(i32)
        place_i = flat2(prob)[:, C:2 * C].bitcast(i32)
        col_place = sb("col_place", [P, 1], i32)
        col_src = sb("col_src", [P, 1], i32)
        col_dst = sb("col_dst", [P, 1], i32)
        col_attr = sb("col_attr", [P, HF])
        z = [xce[b][:].rearrange("p s c f -> p (s c f)").rearrange("p (c h f) -> p c h f", h=H, f=F) for b in (0, 1)]
        cont_f = [sb(f"cont_f{b}", [P, F, COLS[b]]) for b in (0, 1)]
        taken = {"xcm": 0, "sqm": 0}

        def reuse(a, b, name="xcm"):
            at = taken[name]
            taken[name] += a * b
            return flat2({"xcm": xcm, "sqm": sqm}[name])[:, at:at + a * b].rearrange("p (a b) -> p a b", b=b)

        msg = [reuse(F, COLS[b]) for b in (0, 1)]
        run = [reuse(F, COLS[b], "sqm") for b in (0, 1)]
        closed = reuse(F, COLS[0], "sqm").rearrange("p a b -> p (a b)")
        closed_part = sb("closed_part", [P, F])
        run_t = [reuse(COLS[b], F) for b in (0, 1)]
        rows = [reuse(COLS[b], F) for b in (0, 1)]
        ring = [sb(f"ring{b}", [P, COLS[b]], i32) for b in (0, 1)]
        esum = sb("esum", [P, H * COLS[0]])
        rsum = sb("rsum", [P, H * COLS[0]])
        closed_sum = sb("closed_sum", [P, F])
        fix_in = sb("fix_in", [P, F])
        fix_t = sb("fix_t", [F, P])
        fix_rows = sb("fix_rows", [P, F])
        ut = hte[0]

        ps_te = pb("ps_te")
        ps_en = pb("ps_en")
        ps_s = pb("ps_s")
        ps_b = pb("ps_b")
        ps_tm = pb("ps_tm")
        ps_om = [pb(f"ps_om{j}") for j in (0, 1)]
        ps_row = pb("ps_row")

        src_sorted = nc.dram_tensor("src_sorted", [P * C, 1], i32, kind="Internal").ap()
        dst_sorted = nc.dram_tensor("dst_sorted", [P * C, 1], i32, kind="Internal").ap()
        attr_sorted = nc.dram_tensor("attr_sorted", [P * C, HF], fp32, kind="Internal").ap()

        s_zero = sem("s_zero")
        s_pads = sem("s_pads")
        s_before = sem("s_before")
        s_idx = sem("s_idx")
        s_w = sem("s_w")
        s_attr = sem("s_attr")
        s_ident = sem("s_ident")
        s_const = sem("s_const")
        s_blocks = sem("s_blocks")
        s_load = [sem(f"s_load{h}") for h in (0, 1)]
        s_store = [sem(f"s_store{h}") for h in (0, 1)]
        s_flag0 = sem("s_flag0")
        s_downs = sem("s_downs")
        s_down = sem("s_down")
        s_flag = sem("s_flag")
        s_iota = sem("s_iota")
        s_others = sem("s_others")
        s_prep = sem("s_prep")
        s_differ = sem("s_differ")
        s_count = sem("s_count")
        s_piece = sem("s_piece")
        s_place = sem("s_place")
        s_col = sem("s_col")
        s_colscat = sem("s_colscat")
        s_go = sem("s_go")
        s_reload = sem("s_reload")
        s_again = sem("s_again")
        s_setup = sem("s_setup")
        s_bias = sem("s_bias")
        s_whole = sem("s_whole")
        s_ends = sem("s_ends")
        s_rowt = sem("s_rowt")
        s_ring = sem("s_ring")
        s_begun = sem("s_begun")
        s_gather = [sem(f"s_gather{b}") for b in (0, 1)]
        s_kept = sem("s_kept")
        s_esum = sem("s_esum")
        s_ecent = sem("s_ecent")
        s_esq = sem("s_esq")
        s_evar = sem("s_evar")
        s_estd = sem("s_estd")
        s_erstd = sem("s_erstd")
        s_enorm = sem("s_enorm")
        s_mx = sem("s_mx")
        s_shift = sem("s_shift")
        s_watt = sem("s_watt")
        s_score = sem("s_score")
        s_te = sem("s_te")
        s_hte = sem("s_hte")
        s_en = sem("s_en")
        s_s = sem("s_s")
        s_b = sem("s_b")
        s_er = sem("s_er")
        s_base = sem("s_base")
        s_small = sem("s_small")
        s_leak = sem("s_leak")
        s_msum = sem("s_msum")
        s_mcent = sem("s_mcent")
        s_msq = sem("s_msq")
        s_mvar = sem("s_mvar")
        s_mstd = sem("s_mstd")
        s_mrstd = sem("s_mrstd")
        s_mnorm = sem("s_mnorm")
        s_tm = sem("s_tm")
        s_htm = sem("s_htm")
        s_om = sem("s_om")
        s_done = sem("s_done")
        s_left = sem("s_left")
        s_right = sem("s_right")
        s_less = sem("s_less")
        s_exp = sem("s_exp")
        s_floor = sem("s_floor")
        s_recip = sem("s_recip")
        s_alpha = sem("s_alpha")
        s_z = sem("s_z")
        s_ez = sem("s_ez")
        s_zsum = sem("s_zsum")
        s_zr = sem("s_zr")
        s_zn = sem("s_zn")
        s_msg = sem("s_msg")
        s_carried = sem("s_carried")
        s_contf = sem("s_contf")
        s_run = sem("s_run")
        s_runt = sem("s_runt")
        s_cl = sem("s_cl")
        s_cls = sem("s_cls")
        s_fsum = sem("s_fsum")
        s_scidx = sem("s_scidx")
        s_scat = [sem(f"s_scat{b}") for b in (0, 1)]
        s_tu = sem("s_tu")
        s_ut = sem("s_ut")
        s_ou = sem("s_ou")
        s_row = sem("s_row")
        s_fix = sem("s_fix")
        s_fixt = sem("s_fixt")
        s_fixs = sem("s_fixs")
        s_fixed = sem("s_fixed")

        def chunks(engine, body):
            body(0)
            with engine.Fori(1, K) as k:
                body(k)

        def chunks_and_last(engine, body):
            body(0)
            with engine.Fori(1, K - 1) as k:
                body(k)
            body(K - 1)

        def later(k):
            return not isinstance(k, int) or k > 0

        def part(m, h):
            first = isinstance(m, int) and m == 0
            units = range(MS) if h == 0 else range(MS, MU0 if first else MU)
            return units, 2 * m + h, 0 if first else (m - 1) * MU + MU0

        def is_last(k):
            return isinstance(k, int) and k == K - 1

        batches = [(b, i, c, n) for b in (0, 1) for i, (c, n) in enumerate(UNITS[b])]
        unit_no = {(b, i): q for q, (b, i, _, _) in enumerate(batches)}

        THIRD = ((1, 0), (0, COLS[1]))
        assert UNITS[1][0] == UNITS[0][0]
        unit_no3 = {}
        for b, _ in THIRD:
            for i in range(len(UNITS[b])):
                unit_no3[b, i] = len(unit_no3)

        def biased(which):
            c0, c1 = BIAS[which]
            return bias_parts[:, c0:c1]

        def unit_end(k, b):
            return UPC * k + unit_no[b, len(UNITS[b]) - 1] + 1

        block = ctx.enter_context(nc.Block())

        @block.sync
        def _(sp):
            sp.wait_ge(s_zero, 1)
            sp.dma_start(dst_ext[0:P - 1, 1:C + 2], bass.AP(tensor=dst.tensor, offset=dst.offset, ap=[[C, P - 1], [1, C + 1]])
                         ).then_inc(s_idx, 16)
            sp.dma_start(dst_ext[P - 1:P, 1:LASTROW + 1], dst[(P - 1) * C:E].rearrange("(p c) -> p c", p=1)).then_inc(s_idx, 16)
            sp.dma_start(dst_ext[1:P, 0:1], bass.AP(tensor=dst.tensor, offset=dst.offset + C - 1, ap=[[C, P - 1], [1, 1]]),
                         allow_slow_non_contiguous=True).then_inc(s_before, 16)

            def move(n0, u0, u1, out_of_x):
                for p0, p1 in ((0, PA), (PA, PN)):
                    here = xm[p0:p1, u0 * U:u1 * U, :]
                    if out_of_x:
                        sp.dma_start(here, x_n[p0:p1, ds(n0 + u0 * U, (u1 - u0) * U), :]).then_inc(s_load[u0 > 0], 16)
                    else:
                        sp.dma_start(out_n[p0:p1, ds(n0 + u0 * U, (u1 - u0) * U), :], here).then_inc(s_store[u0 > 0], 16)

            move(0, 0, MS, True)
            move(0, MS, MU0, True)
            sp.wait_ge(s_pads, 1)
            for p0, p1, c in ((0, PA, C), (PA, P - 1, C), (P - 1, P, LASTROW)):
                sp.dma_start(er[p0:p1, 0:c, :],
                             r_e[p0 * C:p0 * C + (p1 - p0 - 1) * C + c, :].rearrange("(p c) j -> p c j", c=c)
                             ).then_inc(s_attr, 16)

            def turn(m, n0, units, u_end, more=True):
                for h, (u0, u1) in enumerate(((0, MS), (MS, units))):
                    sp.wait_ge(s_done, u_end - units + u1)
                    move(n0, u0, u1, False)
                    if more:
                        sp.wait_ge(s_store[h], 32 * (m + 1))
                        move(n0 + units * U, u0, u1 if h == 0 else MU, True)
            turn(0, 0, MU0, MU0)
            with sp.Fori(1, K - 1) as m:
                turn(m, (m - 1) * MN + MN0, MU, m * MU + MU0)
            turn(K - 1, (K - 2) * MN + MN0, MU, (K - 1) * MU + MU0, more=False)

        @block.gpsimd
        def _(pool):
            nc.gpsimd.memset(ident[:], 0.0).then_inc(s_ident, 1)
            pool.wait_ge(s_ident, 1)
            nc.gpsimd.affine_select(out=ident[:], in_=ident[:], compare_op=ALU.not_equal, fill=1.0, base=0,
                                    pattern=[[-1, P]], channel_multiplier=1).then_inc(s_ident, 1)

            pool.wait_ge(s_flag, 1)
            flag = pool.value_load(unsorted[0:1, 0:1], min_val=0, max_val=1)
            with pool.If(flag != 0):
                nc.gpsimd.iota(iota_i, pattern=[[1, C]], base=0, channel_multiplier=C).then_inc(s_iota, 1)
                nc.gpsimd.iota(iota_o, pattern=[[1, PIECE]], base=0, channel_multiplier=0).then_inc(s_iota, 1)
                with pool.Fori(0, PIECES) as j:
                    nc.gpsimd.dma_start(others, dst[ds(j * PIECE, PIECE)].rearrange("(a c) -> a c", a=1).to_broadcast([P, PIECE])
                                        ).then_inc(s_others, 16)
                    pool.wait_ge(s_piece, j + 1)
                    pool.sem_inc(s_go, 1)
                with pool.Fori(0, C) as c:
                    pool.wait_ge(s_col, 4 * c + 4)
                    pool.sem_inc(s_go, 1)
                    for sorted_, col in ((src_sorted, col_src[:]), (dst_sorted, col_dst[:]), (attr_sorted, col_attr[:])):
                        nc.gpsimd.indirect_dma_start(sorted_, bass.IndirectOffsetOnAxis(ap=col_place[:], axis=0), col, None,
                                                     bounds_check=P * C - 1, oob_is_err=False).then_inc(s_colscat, 16)
                pool.wait_ge(s_colscat, 3 * 16 * C)
                pool.wait_ge(s_before, 16)
                rows_of = lambda v, w: v.rearrange("(p c) w -> p (c w)", p=P)
                nc.gpsimd.dma_start(src_idx[:, 0:C], rows_of(src_sorted, 1)).then_inc(s_reload, 16)
                nc.gpsimd.dma_start(flat2(er), rows_of(attr_sorted, HF)).then_inc(s_reload, 16)
                one = lambda a, b: dst_sorted[a:b, :].rearrange("(p c) w -> p (c w)", p=1)
                nc.gpsimd.dma_start(dst_ext[0:1, 1:C + 2], one(0, C + 1)).then_inc(s_reload, 16)
                nc.gpsimd.dma_start(dst_ext[P - 1:P, 0:C + 1], one((P - 1) * C - 1, P * C)).then_inc(s_reload, 16)
                nc.gpsimd.dma_start(dst_ext[1:P - 1, 0:C + 2],
                                    bass.AP(tensor=dst_sorted.tensor, offset=dst_sorted.offset + C - 1, ap=[[C, P - 2], [1, C + 2]])
                                    ).then_inc(s_reload, 16)
                pool.wait_ge(s_again, 2)

            def gather(k):
                for b in (0, 1):
                    pool.wait_ge(s_ring, 2 * k + b + 1)
                    if later(k):
                        pool.wait_ge(s_ecent, 2 * k + b - 1)
                        pool.wait_ge(s_kept, 2 * k + b - 1)
                    pool.sem_inc(s_begun, 1)
                    for j in range(COLS[b]):
                        for side, idx in ((0, idx_s[b]), (1, idx_d[b])):
                            nc.gpsimd.indirect_dma_start(
                                xe[b][:, side, j, :], None, x,
                                bass.IndirectOffsetOnAxis(ap=idx[:, j:j + 1], axis=0)).then_inc(s_gather[b], 16)
            chunks(pool, gather)

            for h in (0, 1):
                pool.wait_ge(s_store[h], 32 * K)

            def scatter(k):
                for place3, (b, _) in enumerate(THIRD):
                    pool.wait_ge(s_scidx, 2 * k + place3 + 1)
                    for i, (c, m) in enumerate(UNITS[b]):
                        pool.wait_ge(s_row, UPC * k + unit_no3[b, i] + 1)
                        pool.sem_inc(s_begun, 1)
                        for j in range(c, c + m):
                            nc.gpsimd.indirect_dma_start(
                                out, bass.IndirectOffsetOnAxis(ap=ring[b][:, j:j + 1], axis=0),
                                rows[b][:, j, :], None, bounds_check=N - 1, oob_is_err=False).then_inc(s_scat[b], 16)
            chunks(pool, scatter)
            pool.wait_ge(s_fixs, 1)
            nc.gpsimd.indirect_dma_start(
                out, bass.IndirectOffsetOnAxis(ap=fix_idx[:], axis=0), fix_rows[:], None,
                bounds_check=N - 1, oob_is_err=False).then_inc(s_fixed, 16)
            for b in (0, 1):
                pool.wait_ge(s_scat[b], 16 * COLS[b] * K)
            pool.wait_ge(s_fixed, 16)

        @block.scalar
        def _(act):
            act.wait_ge(s_zero, 1)
            act.dma_start(src_idx[0:P - 1, 0:C], src[0:(P - 1) * C].rearrange("(p c) -> p c", c=C)).then_inc(s_idx, 16)
            act.dma_start(src_idx[P - 1:P, 0:LASTROW], src[(P - 1) * C:E].rearrange("(p c) -> p c", p=1)).then_inc(s_idx, 16)
            act.wait_ge(s_zero, 2)
            nc.scalar.activation(er[96:P, LASTROW:C, :], zeros[96:P, :].rearrange("p (a j) -> p a j", a=1
                                                                                ).to_broadcast([P - 96, C - LASTROW, HF]),
                                 ACT.Copy).then_inc(s_pads, 1)
            for dest, w in zip(w_all, (W2s, W2d, W1)):
                act.dma_start(dest[:], bass.AP(tensor=w.tensor, offset=w.offset, ap=[[0, G], [w.shape[1], F], [1, w.shape[1]]])
                              ).then_inc(s_w, 16)
            for dest, v in ((bias[:, 0:G * HF], b2s), (b2d_row[:], b2d), (bias[:, 2 * G * HF:NB], b1)):
                m = v.shape[0]
                act.dma_start(dest, bass.AP(tensor=v.tensor, offset=v.offset, ap=[[0, P], [0, G], [1, m]])).then_inc(s_w, 16)
            act.dma_start(attn_all[:], attn.rearrange("a h f -> a (h f)").to_broadcast([P, HF])).then_inc(s_w, 16)
            act.wait_ge(s_const, 1)
            act.wait_ge(s_w, WEIGHT_DMAS)
            for dest, w in zip((w2s_blocks, w2d_blocks, w1_blocks), w_all):
                m = w.shape[1]
                for c in range(G):
                    nc.scalar.activation(dest[c * F:(c + 1) * F, c * m:(c + 1) * m], w[c * F:(c + 1) * F, :], ACT.Copy
                                         ).then_inc(s_blocks, 1)

            def rows_of(buffer, units):
                return buffer[0:PN, units[0] * U:(units[-1] + 1) * U]

            def node_square(m, h):
                units, before, _ = part(m, h)
                act.wait_ge(s_mcent, before + 1)
                nc.scalar.activation(rows_of(sqm, units), rows_of(xcm, units), ACT.Square).then_inc(s_msq, 1)

            def node_sqrt(m, h):
                units, before, _ = part(m, h)
                act.wait_ge(s_mvar, before + 1)
                nc.scalar.activation(rows_of(stdm, units), rows_of(varm, units), ACT.Sqrt, scale=1.0 / F,
                                     bias=eps[0:PN, :]).then_inc(s_mstd, 1)

            def node_relu(m, h):
                units, _, u0 = part(m, h)
                for j in units:
                    act.wait_ge(s_tm, u0 + j + 1)
                    if not isinstance(u0, int) or u0 + j - 1 > 0:
                        act.wait_ge(s_om, u0 + j - (j > 0))
                    nc.scalar.activation(htm[j % 2][:], ps_tm[:, 0:4 * PN], ACT.Relu).then_inc(s_htm, 1)

            def edge_relu(k, b, i):
                c, n = UNITS[b][i]
                q = UPC * k + unit_no[b, i]
                act.wait_ge(s_te, q + 1)
                if later(k) or unit_no[b, i] > 1:
                    act.wait_ge(s_b, q - 1)
                nc.scalar.activation(hte[unit_no[b, i] % 2][:, 0:n * 2 * F], ps_te[:, 0:n * 2 * F], ACT.Relu).then_inc(s_hte, 1)

            def edge_small(k, b, i):
                c, n = UNITS[b][i]
                q = UPC * k + unit_no[b, i]
                act.wait_ge(s_s, q + 1)
                if later(k) or unit_no[b, i]:
                    act.wait_ge(s_leak, q)
                nc.scalar.activation(small_s[:, 0:n * HF], ps_s[:, 0:n * HF], ACT.Copy,
                                     scale=SLOPE).then_inc(s_small, 1)

            for step_ in (node_square, node_sqrt, node_relu):
                for h in (0, 1):
                    step_(0, h)

            def chunk(k):
                for b in (0, 1):
                    t = 2 * k + b + 1
                    act.wait_ge(s_gather[b], 16 * 2 * COLS[b] * (k + 1))
                    nc.scalar.activation(base[:, ds(k * CC + OFF[b], COLS[b]), :], xe[b][:, 1, :, :],
                                         ACT.Copy).then_inc(s_kept, 1)
                    act.wait_ge(s_ecent, t)
                    nc.scalar.activation(sqe[b][:], xce[b][:], ACT.Square).then_inc(s_esq, 1)
                    act.wait_ge(s_evar, t)
                    nc.scalar.activation(stde[:, 0:2 * COLS[b]], vare[:, 0:2 * COLS[b]], ACT.Sqrt, scale=1.0 / F,
                                         bias=eps[:]).then_inc(s_estd, 1)
                    assert len(UNITS[b]) == 2
                    nodes = not is_last(k)
                    if nodes:
                        node_square(k + 1, b)
                    edge_relu(k, b, 0)
                    edge_relu(k, b, 1)
                    if nodes:
                        node_sqrt(k + 1, b)
                    edge_small(k, b, 0)
                    edge_small(k, b, 1)
                    if nodes:
                        node_relu(k + 1, b)
            chunks_and_last(act, chunk)

            for h in range(H):
                act.wait_ge(s_less, h + 1)
                nc.scalar.activation(prob[:, h, :], prob[:, h, :], ACT.Exp).then_inc(s_exp, 1)

            def third(k):
                for place3, (b, off) in enumerate(THIRD):
                    t = 2 * k + place3 + 1
                    if later(k):
                        act.wait_ge(s_run, t - 2)
                    nc.scalar.activation(
                        cont_f[b][:, :, 1:COLS[b]],
                        cont[:, ds(k * CC + off + 1, COLS[b] - 1)].rearrange("p (a c) -> p a c", a=1).to_broadcast([P, F, COLS[b] - 1]),
                        ACT.Copy).then_inc(s_contf, 1)
                    act.wait_ge(s_z, t)
                    nc.scalar.activation(z[b], z[b], ACT.Exp).then_inc(s_ez, 1)
                    act.wait_ge(s_run, t)
                    nc.scalar.activation(run_t[b], run[b][:].rearrange("p f c -> p c f"), ACT.Copy).then_inc(s_runt, 1)
                    for i, (c, n) in enumerate(UNITS[b]):
                        q = UPC * k + unit_no3[b, i]
                        act.wait_ge(s_tu, q + 1)
                        if later(k) or unit_no3[b, i]:
                            act.wait_ge(s_ou, q)
                        nc.scalar.activation(ut[:, 0:n * F], ps_te[:, 0:n * F], ACT.Copy).then_inc(s_ut, 1)
            chunks(act, third)

        @block.tensor
        def _(pe):
            pe.wait_ge(s_downs, 1)
            nc.tensor.matmul(ps_row[0:1, 0:1], downs[:], ones_col[:], start=True, stop=True).then_inc(s_down, 1)
            pe.wait_ge(s_ident, 2)

            def node_units(m, h):
                units, before, u0 = part(m, h)
                pe.wait_ge(s_mnorm, before + 1)

                def transposes(j):
                    if not isinstance(u0, int) or u0 + j > 0:
                        pe.wait_ge(s_htm, u0 + j)
                    for g in range(4):
                        a = j * U + g * G
                        m = nc.tensor.transpose(ps_tm[:, g * PN:(g + 1) * PN],
                                                xcm[0:PN, a:a + G, :].rearrange("p a f -> p (a f)"),
                                                ident[0:PN, 0:PN])
                    m.then_inc(s_tm, 1)

                transposes(units[0])
                for j in units:
                    if j < units[-1]:
                        transposes(j + 1)
                    if not isinstance(u0, int) or u0 + j > 1:
                        pe.wait_ge(s_done, u0 + j - (j > 0))
                    pe.wait_ge(s_htm, u0 + j + 1)
                    for g in range(4):
                        o = ps_om[j % 2][0:PN, g * P:(g + 1) * P]
                        nc.tensor.matmul(o, ones[:, 0:PN], biased("b1"), start=True, stop=False)
                        m = nc.tensor.matmul(o, htm[j % 2][:, g * PN:(g + 1) * PN], w1_blocks[:], start=False, stop=True)
                    m.then_inc(s_om, 1)

            pe.wait_ge(s_whole, 2)
            for w in (0, 1):
                m = nc.tensor.transpose(ps_row[0:F, w * P:(w + 1) * P], whole[:, w, :], ident[:])
            m.then_inc(s_rowt, 1)
            pe.wait_ge(s_blocks, 3 * G)
            pe.wait_ge(s_const, 2)
            pe.wait_ge(s_bias, BIAS_STEPS)
            for h in (0, 1):
                node_units(0, h)

            def edge_transposes(k, b, i):
                c, n = UNITS[b][i]
                q = UPC * k + unit_no[b, i]
                if later(k) or unit_no[b, i]:
                    pe.wait_ge(s_hte, q)
                for g in range(n // G):
                    for side in (0, 1):
                        m = nc.tensor.transpose(ps_te[:, (2 * g + side) * P:(2 * g + side + 1) * P],
                                                xce[b][:, side, c + g * G:c + (g + 1) * G, :].rearrange("p c f -> p (c f)"), ident[:])
                m.then_inc(s_te, 1)

            def warm_up():
                for _ in range(WARM_UPS):
                    nc.tensor.matmul(ps_row[:, 0:G * HF], ones[:], biased("b2s"), start=True, stop=True)

            def chunk(k):
                for b in (0, 1):
                    if is_last(k) and b == 1:
                        pe.wait_ge(s_esum, 2 * K)
                        warm_up()
                    pe.wait_ge(s_enorm, 2 * k + b + 1)
                    edge_transposes(k, b, 0)
                    for i, (c, n) in enumerate(UNITS[b]):
                        q = UPC * k + unit_no[b, i]
                        again = later(k) or unit_no[b, i]
                        if i + 1 < len(UNITS[b]):
                            edge_transposes(k, b, i + 1)
                        pe.wait_ge(s_hte, q + 1)
                        if again:
                            pe.wait_ge(s_leak, q)
                        ht = hte[unit_no[b, i] % 2]
                        hs = [ht[:, 2 * g * P:(2 * g + 1) * P] for g in range(n // G)]
                        hd = [ht[:, (2 * g + 1) * P:(2 * g + 2) * P] for g in range(n // G)]

                        def products(ps, m, which, factors):
                            for g in range(n // G):
                                o = ps[:, g * G * m:(g + 1) * G * m]
                                nc.tensor.matmul(o, ones[:], biased(which), start=True, stop=False)
                                for f, (rows_t, w) in enumerate(factors):
                                    last_mm = nc.tensor.matmul(o, rows_t[g], w[:], start=False, stop=f == len(factors) - 1)
                            return last_mm

                        products(ps_s, HF, "b2sd", ((hs, w2s_blocks), (hd, w2d_blocks))).then_inc(s_s, 1)
                        if again:
                            pe.wait_ge(s_er, q)
                        products(ps_en, HF, "b2s", ((hs, w2s_blocks),)).then_inc(s_en, 1)
                        if again:
                            pe.wait_ge(s_base, q)
                        products(ps_b, F, "b1", ((hd, w1_blocks),)).then_inc(s_b, 1)
                    if not is_last(k):
                        node_units(k + 1, b)
            chunks_and_last(pe, chunk)

            for r, (left, right) in enumerate(((left_max, right_max), (left_sum, right_sum))):
                pe.wait_ge(s_ends, 6 * r + 2)
                nc.tensor.transpose(ps_row[0:H, 0:P], fwd[:, :, C - 1], ident[:]).then_inc(s_rowt, 1)
                pe.wait_ge(s_ends, 6 * r + 4)
                nc.tensor.transpose(ps_en[0:H, 0:P], bwd[:, :, 0], ident[:]).then_inc(s_rowt, 1)
                pe.wait_ge(s_ends, 6 * r + 5)
                nc.tensor.transpose(ps_s[:, 0:H], left[0:H, 0:P], ident[0:H, 0:H])
                pe.wait_ge(s_ends, 6 * r + 6)
                nc.tensor.transpose(ps_s[:, H:2 * H], right[0:H, 1:P + 1], ident[0:H, 0:H]).then_inc(s_rowt, 1)

            def third(k):
                for place3, (b, _) in enumerate(THIRD):
                    pe.wait_ge(s_runt, 2 * k + place3 + 1)
                    for i, (c, n) in enumerate(UNITS[b]):
                        q = UPC * k + unit_no3[b, i]
                        again = later(k) or unit_no3[b, i]
                        if again:
                            pe.wait_ge(s_ut, q)
                        for g in range(n // G):
                            m = nc.tensor.transpose(ps_te[:, g * P:(g + 1) * P],
                                                    run_t[b][:, c + g * G:c + (g + 1) * G, :].rearrange("p c f -> p (c f)"),
                                                    ident[:])
                        m.then_inc(s_tu, 1)
                        pe.wait_ge(s_ut, q + 1)
                        if again:
                            pe.wait_ge(s_row, q)
                        for g in range(n // G):
                            m = nc.tensor.matmul(ps_b[:, g * G * F:(g + 1) * G * F], ut[:, g * P:(g + 1) * P],
                                                 w1_blocks[:], start=True, stop=True)
                        m.then_inc(s_ou, 1)
            chunks(pe, third)

            nc.tensor.transpose(ps_row[0:F, 0:P], run[0][:, :, COLS[0] - 1], ident[:]).then_inc(s_fixt, 1)
            pe.wait_ge(s_fix, 1)
            nc.tensor.transpose(ps_row[:, P:P + F], left_sum[:, 0:P], ident[0:F, 0:F]).then_inc(s_fixt, 1)
            pe.wait_ge(s_fix, 2)
            nc.tensor.transpose(ps_row[0:F, 2 * P:3 * P], fix_in[:], ident[:]).then_inc(s_fixt, 1)
            pe.wait_ge(s_fix, 3)
            nc.tensor.matmul(ps_row[:, 3 * P:3 * P + F], fix_t[:], w1_blocks[0:F, 0:F], start=True, stop=True).then_inc(s_fixt, 1)

        @block.vector
        def _(dve):
            V = nc.vector
            V.memset(src_idx[96:P, LASTROW:C], 0)
            V.memset(dst_ext[0:1, 0:1], NOWHERE)
            V.memset(dst_ext[96:P, LASTROW:C + 2], NOWHERE).then_inc(s_zero, 1)
            V.memset(zeros[:], 0.0).then_inc(s_zero, 1)
            V.memset(ones_col[:], 1.0)
            V.memset(eps[:], EPS)
            V.memset(w2s_blocks[:], 0.0)
            V.memset(w2d_blocks[:], 0.0)
            V.memset(w1_blocks[:], 0.0).then_inc(s_const, 1)
            V.memset(bias_parts[:], 0.0)
            for b in (0, 1):
                V.memset(cont_f[b][:, :, 0:1], 0.0)
            V.memset(closed_sum[:], 0.0)
            V.memset(left_max[:, 0:1], -BIG)
            V.memset(left_sum[:, 0:1], 0.0)
            V.memset(right_max[:, P:P + 1], -BIG)
            V.memset(right_sum[:, P:P + 1], 0.0)
            V.memset(ones[:], 1.0).then_inc(s_const, 1)

            def indices(k, b):
                c = k * CC + OFF[b]
                V.tensor_copy(idx_s[b][:], src_idx[:, ds(c, COLS[b])])
                return V.tensor_scalar(idx_d[b][:], dst_ext[:, ds(c + 1, COLS[b])], float(N - 1), None, ALU.min)

            dve.wait_ge(s_idx, 16 * 4)
            V.tensor_tensor(down[:], dst_ext[:, 1:C + 1], dst_ext[:, 2:C + 2], ALU.is_gt).then_inc(s_flag0, 1)
            dve.wait_ge(s_flag0, 1)
            V.reduce_sum(downs[:], down[:], AX.X).then_inc(s_downs, 1)
            for b in (0, 1):
                indices(0, b).then_inc(s_ring, 1)
            dve.wait_ge(s_down, 1)
            V.tensor_scalar(unsorted[:], ps_row[0:1, 0:1], 1.0, None, ALU.min).then_inc(s_flag, 1)
            dve.wait_ge(s_flag, 1)

            flag = dve.value_load(unsorted[0:1, 0:1], min_val=0, max_val=1)
            with dve.If(flag != 0):
                dve.wait_ge(s_attr, 48)
                dve.wait_ge(s_iota, 2)
                prepared = [0]

                def prepare(ins):
                    prepared[0] += 1
                    ins.then_inc(s_prep, 1)
                    dve.wait_ge(s_prep, prepared[0])

                prepare(V.tensor_copy(own_no, iota_i))
                prepare(V.tensor_copy(others_no, iota_o))
                prepare(V.tensor_scalar(own_key, dst_ext[:, 1:C + 1], float(KEY), None, ALU.mult))
                prepare(V.tensor_scalar(smaller, dst_ext[:, 1:C + 1], float(N), None, ALU.is_ge))
                prepare(V.scalar_tensor_tensor(place, own_no, -float(E), smaller, ALU.add, ALU.mult))
                PREPARED = prepared[0]
                with V.Fori(0, PIECES) as j:
                    dve.wait_ge(s_others, 16 * j + 16)
                    V.tensor_scalar(others_key, others, float(KEY), None, ALU.mult).then_inc(s_prep, 1)
                    with V.Fori(0, C) as c:
                        dve.wait_ge(s_prep, PREPARED + 1 + 2 * j)
                        V.scalar_tensor_tensor(differ, others_key, own_key[:, ds(c, 1)], others_no,
                                               ALU.subtract, ALU.add).then_inc(s_differ, 1)
                        dve.wait_ge(s_differ, j * C + c + 1)
                        V.tensor_scalar(differ, differ, own_no[:, ds(c, 1)], None, ALU.is_lt, ALU.add,
                                        accum_out=smaller[:, ds(c, 1)]).then_inc(s_count, 1)
                        dve.wait_ge(s_count, j * C + c + 1)
                    V.tensor_tensor(place, place, smaller, ALU.add).then_inc(s_prep, 1)
                    dve.wait_ge(s_prep, PREPARED + 2 + 2 * j)
                    V.tensor_scalar(own_no, own_no, -float(PIECE), None, ALU.add).then_inc(s_piece, 1)
                    dve.wait_ge(s_piece, j + 1)
                V.tensor_copy(place_i, place).then_inc(s_place, 1)
                dve.wait_ge(s_place, 1)
                with V.Fori(0, C) as c:
                    for to, of in ((col_place, place_i), (col_src, src_idx), (col_dst, dst_ext[:, 1:])):
                        V.tensor_copy(to[:], of[:, ds(c, 1)]).then_inc(s_col, 1)
                    V.tensor_copy(col_attr[:], er[:, ds(c, 1), :].rearrange("p a j -> p (a j)")).then_inc(s_col, 1)
                    dve.wait_ge(s_colscat, 48 * c + 48)
                dve.wait_ge(s_reload, 16 * 5)
                for b in (0, 1):
                    indices(0, b).then_inc(s_again, 1)

            count = [0]

            def step(ins):
                count[0] += 1
                ins.then_inc(s_setup, 1)
                dve.wait_ge(s_setup, count[0])

            dve.wait_ge(s_before, 16)
            step(V.tensor_copy(dst_f[:], dst_ext[:, 0:C + 2]))
            here = dst_f[:, 1:C + 1]
            step(V.tensor_scalar(real[:], here, float(N), None, ALU.is_lt))
            step(V.tensor_tensor(cont[:], here, dst_f[:, 0:C], ALU.is_equal))
            step(V.tensor_tensor(cnext[:], here, dst_f[:, 2:C + 2], ALU.is_equal))
            step(V.tensor_tensor(cont[:], cont[:], real[:], ALU.mult))
            step(V.tensor_tensor(cnext[:], cnext[:], real[:], ALU.mult))
            step(V.tensor_scalar(last[:], cnext[:], -1.0, 1.0, ALU.mult, ALU.add))
            step(V.tensor_tensor_scan(head[:], cont[:], cont[:], 1.0, ALU.mult, ALU.mult))
            step(V.tensor_tensor_scan(tail[:, ::-1], cnext[:, ::-1], cnext[:, ::-1], 1.0, ALU.mult, ALU.mult))
            V.tensor_copy(whole[:, 0, :], head[:, C - 1:C].to_broadcast([P, F])).then_inc(s_whole, 1)
            V.tensor_copy(whole[:, 1, :], tail[:, 0:1].to_broadcast([P, F])).then_inc(s_whole, 1)
            step(V.tensor_scalar(reset[:], cont[:], -1.0, BIG, ALU.add, ALU.mult))
            step(V.tensor_scalar(reset_next[:], cnext[:], -1.0, BIG, ALU.add, ALU.mult))
            step(V.tensor_scalar(reset_head[:], head[:], -1.0, BIG, ALU.add, ALU.mult))
            step(V.tensor_scalar(reset_tail[:], tail[:], -1.0, BIG, ALU.add, ALU.mult))
            step(V.tensor_tensor(close[:], last[:], head[:], ALU.mult))
            step(V.tensor_tensor(keep[:], last[:], close[:], ALU.subtract))
            step(V.scalar_tensor_tensor(moved[:], here, float(NOWHERE), keep[:], ALU.subtract, ALU.mult))
            step(V.tensor_scalar(scat_idx[:], moved[:], float(NOWHERE), None, ALU.add))
            step(V.scalar_tensor_tensor(moved[:], here, float(NOWHERE), close[:], ALU.subtract, ALU.mult))
            step(V.reduce_sum(fix_f[:], moved[:], AX.X))
            step(V.tensor_scalar(fix_idx[:], fix_f[:], float(NOWHERE), None, ALU.add))

            def over(v):
                return v.rearrange("p (a b) -> p a b", b=1).to_broadcast([*v.shape, F])

            def node_norm(m, h):
                units, before, _ = part(m, h)
                t, n = before + 1, len(units) * U
                span = slice(units[0] * U, units[0] * U + n)
                a, ac, sq = (v[0:PN, span, :] for v in (xm, xcm, sqm))
                total, var, std, rstd = (v[0:PN, span] for v in (summ, varm, stdm, rstdm))
                dve.wait_ge(s_load[h], 32 * (m + 1))
                V.reduce_sum(total, a, AX.X).then_inc(s_msum, 1)
                yield
                dve.wait_ge(s_msum, t)
                V.scalar_tensor_tensor(ac, over(total), -1.0 / F, a, ALU.mult, ALU.add).then_inc(s_mcent, 1)
                yield
                dve.wait_ge(s_msq, t)
                V.reduce_sum(var, sq, AX.X).then_inc(s_mvar, 1)
                yield
                dve.wait_ge(s_mstd, t)
                V.reciprocal(rstd, std).then_inc(s_mrstd, 1)
                dve.wait_ge(s_mrstd, t)
                V.tensor_tensor(ac, ac, over(rstd), ALU.mult).then_inc(s_mnorm, 1)
                yield

            def node_add(m, h, j):
                _, _, u0 = part(m, h)
                o = xm[0:PN, j * U:(j + 1) * U, :].rearrange("p a f -> p (a f)")
                dve.wait_ge(s_om, u0 + j + 1)
                V.tensor_tensor(o, ps_om[j % 2][0:PN, :], o, ALU.add).then_inc(s_done, 1)

            steps = [0]

            def split(ins):
                steps[0] += 1
                ins.then_inc(s_bias, 1)
                dve.wait_ge(s_bias, steps[0])

            dve.wait_ge(s_rowt, 1)
            step(V.tensor_copy(whole_row[:].rearrange("f w p -> f (w p)"), ps_row[0:F, 0:2 * P]))
            step(V.tensor_scalar(reset_row[:], whole_row[:], -1.0, BIG, ALU.add, ALU.mult))
            first, second = node_norm(0, 0), node_norm(0, 1)
            next(first)
            next(first)
            next(second)
            next(second)
            dve.wait_ge(s_w, WEIGHT_DMAS)
            c0, c1 = BIAS["b2sd"]
            split(V.tensor_tensor(bias[:, c0:c1], bias[:, 0:c0], b2d_row[:], ALU.add))
            for i, of in ((0, bias), (1, bias_rest), (2, bias_rest)):
                split(V.tensor_copy(bias_part[:, i, :], of[:]))
                if i < 2:
                    split(V.tensor_tensor(bias_rest[:], of[:], bias_part[:, i, :], ALU.subtract))
            for i, p in enumerate(PARTS):
                split(V.tensor_copy(bias_parts[p:p + 1, :], bias_part[p:p + 1, i, :]))
            assert steps[0] == BIAS_STEPS
            for nodes in (first, second):
                for _ in nodes:
                    pass
            for j in range(MU0):
                node_add(0, int(j >= MS), j)
            dve.wait_ge(s_attr, 48)

            def edge_norm(k, b):
                t, n = 2 * k + b + 1, COLS[b]
                a = xe[b][:].rearrange("p s c f -> p (s c) f")
                ac = xce[b][:].rearrange("p s c f -> p (s c) f")
                sq = sqe[b][:].rearrange("p s c f -> p (s c) f")
                dve.wait_ge(s_gather[b], 16 * 2 * n * (k + 1))
                if not is_last(k):
                    indices(k + 1, b).then_inc(s_ring, 1)
                V.reduce_sum(sume[:, 0:2 * n], a, AX.X).then_inc(s_esum, 1)
                dve.wait_ge(s_esum, t)
                V.scalar_tensor_tensor(ac, over(sume[:, 0:2 * n]), -1.0 / F, a, ALU.mult, ALU.add).then_inc(s_ecent, 1)
                yield
                dve.wait_ge(s_esq, t)
                V.reduce_sum(vare[:, 0:2 * n], sq, AX.X).then_inc(s_evar, 1)
                yield
                dve.wait_ge(s_estd, t)
                V.reciprocal(rstde[:, 0:2 * n], stde[:, 0:2 * n]).then_inc(s_erstd, 1)
                dve.wait_ge(s_erstd, t)
                V.tensor_tensor(ac, ac, over(rstde[:, 0:2 * n]), ALU.mult).then_inc(s_enorm, 1)
                yield

            def edge_unit(k, b, i):
                c, m = UNITS[b][i]
                q = UPC * k + unit_no[b, i]
                cols = ds(k * CC + OFF[b] + c, m)
                flat = lambda v: v.rearrange("p c j -> p (c j)")
                dve.wait_ge(s_small, q + 1)
                V.tensor_tensor(flat(leak[b][:, c:c + m, :]), ps_s[:, 0:m * HF], small_s[:, 0:m * HF],
                                ALU.max).then_inc(s_leak, 1)
                dve.wait_ge(s_en, q + 1)
                V.tensor_tensor(flat(er[:, cols, :]), ps_en[:, 0:m * HF], flat(er[:, cols, :]),
                                ALU.mult).then_inc(s_er, 1)
                dve.wait_ge(s_b, q + 1)
                dve.wait_ge(s_kept, 2 * k + b + 1)
                V.tensor_tensor(flat(base[:, cols, :]), ps_b[:, 0:m * F], flat(base[:, cols, :]), ALU.add).then_inc(s_base, 1)

            def edge_score(k, b, only_score=False):
                t, n = 2 * k + b + 1, COLS[b]
                cols = ds(k * CC + OFF[b], n)
                dve.wait_ge(s_base, unit_end(k, b))
                V.tensor_tensor(leak[b][:], leak[b][:], attn_all[:].rearrange("p (a j) -> p a j", a=1).to_broadcast([P, n, HF]),
                                ALU.mult).then_inc(s_watt, 1)
                if not only_score:
                    edge_max(k, b)
                dve.wait_ge(s_watt, t)
                V.reduce_sum(score[:, :, cols].rearrange("p h c -> p c h"), leak[b][:].rearrange("p c (h f) -> p c h f", h=H),
                             AX.X).then_inc(s_score, 1)
                if not only_score:
                    edge_shift(k, b)

            def edge_products(k, b):
                return er[:, ds(k * CC + OFF[b], COLS[b]), :].rearrange("p c (h f) -> p (c h) f", h=H)

            def edge_max(k, b):
                V.reduce_max(mxe[:, 0:H * COLS[b]], edge_products(k, b), AX.X).then_inc(s_mx, 1)

            def edge_shift(k, b):
                dve.wait_ge(s_mx, 2 * k + b + 1)
                rr = edge_products(k, b)
                V.tensor_tensor(rr, rr, over(mxe[:, 0:H * COLS[b]]), ALU.subtract).then_inc(s_shift, 1)

            def chunk(k):
                for b in (0, 1):
                    edges = edge_norm(k, b)
                    nodes = node_norm(k + 1, b) if not is_last(k) else iter(range(4))
                    m, h = (k, 1) if b == 0 else (k + 1, 0)
                    done = part(m, h)[0] if (later(k) if b == 0 else not is_last(k)) else range(0)
                    for j in done[:2]:
                        node_add(m, h, j)
                    next(edges)
                    next(nodes)
                    for j in done[2:]:
                        node_add(m, h, j)
                    next(edges)
                    next(nodes)
                    next(edges)
                    next(nodes)
                    next(nodes)
                    for i in range(len(UNITS[b])):
                        edge_unit(k, b, i)
                    edge_score(k, b, only_score=is_last(k) and b == 1)
            chunks_and_last(V, chunk)

            V.memset(run[0][:, :, COLS[0] - 1:COLS[0]], 0.0)
            dve.wait_ge(s_score, 2 * K)

            def less(h):
                dve.wait_ge(s_right, h + 1)
                V.tensor_tensor(prob[:, h, :], score[:, h, :], full[:, h, :], ALU.subtract).then_inc(s_less, 1)

            for r, (values, first, from_before, from_behind, from_left, from_right, row_flags, left, right, op, row_op) in enumerate((
                    (score, -BIG, reset, reset_next, reset_head, reset_tail, reset_row, left_max, right_max, ALU.add, ALU.max),
                    (prob, 0.0, cont, cnext, head, tail, whole_row, left_sum, right_sum, ALU.mult, ALU.add))):
                for h in range(H):
                    if r == 1:
                        dve.wait_ge(s_exp, h + 1)
                    V.tensor_tensor_scan(fwd[:, h, :], from_before[:], values[:, h, :], first, op, row_op).then_inc(s_ends, 1)
                for h in range(H):
                    V.tensor_tensor_scan(bwd[:, h, ::-1], from_behind[:, ::-1], values[:, h, ::-1], first, op, row_op).then_inc(s_ends, 1)
                dve.wait_ge(s_rowt, 3 * r + 2)
                V.tensor_tensor_scan(left[0:H, 1:P + 1], row_flags[0:H, 0, :], ps_row[0:H, 0:P], first, op, row_op).then_inc(s_ends, 1)
                dve.wait_ge(s_rowt, 3 * r + 3)
                V.tensor_tensor_scan(right[0:H, P - 1::-1], row_flags[0:H, 1, ::-1], ps_en[0:H, P - 1::-1], first,
                                     op, row_op).then_inc(s_ends, 1)
                step(V.tensor_tensor(full[:], fwd[:], bwd[:], row_op))
                if r == 1:
                    step(V.tensor_tensor(full[:], full[:], prob[:], ALU.subtract))
                dve.wait_ge(s_rowt, 3 * r + 4)
                step(V.tensor_copy(carry[r][:].rearrange("p w h -> p (w h)"), ps_s[:, 0:2 * H]))
                for h in range(H):
                    V.scalar_tensor_tensor(full[:, h, :], from_left[:], carry[r][:, 0, h:h + 1], full[:, h, :], op, row_op
                                           ).then_inc(s_left, 1)
                dve.wait_ge(s_left, H * (r + 1))
                for h in range(H):
                    V.scalar_tensor_tensor(full[:, h, :], from_right[:], carry[r][:, 1, h:h + 1], full[:, h, :], op, row_op
                                           ).then_inc(s_right, 1)
                    if r == 0 and h > 0:
                        less(h - 1)
                if r == 0:
                    less(H - 1)
                    edge_max(K - 1, 1)
            dve.wait_ge(s_right, 2 * H)
            edge_shift(K - 1, 1)
            dve.wait_ge(s_shift, 2 * K)

            def third(k):
                for place3, (b, off) in enumerate(THIRD):
                    t = 2 * k + place3 + 1
                    n, m_before = COLS[b], COLS[1 - b]
                    cols = ds(k * CC + off, n)
                    e4 = z[b]
                    e3 = z[b].rearrange("p c h f -> p (c h) f")
                    V.tensor_scalar(alpha[b][:], full[:, :, cols], 1e-9, None, ALU.max).then_inc(s_floor, 1)
                    dve.wait_ge(s_floor, t)
                    V.reciprocal(alpha[b][:], alpha[b][:]).then_inc(s_recip, 1)
                    dve.wait_ge(s_recip, t)
                    V.tensor_tensor(alpha[b][:], alpha[b][:], prob[:, :, cols], ALU.mult).then_inc(s_alpha, 1)
                    dve.wait_ge(s_alpha, t)
                    V.tensor_tensor(e4, er[:, cols, :].rearrange("p c (h f) -> p c h f", h=H),
                                    alpha[b][:].rearrange("p h (c a) -> p c h a", a=1).to_broadcast([P, n, H, F]),
                                    ALU.mult).then_inc(s_z, 1)
                    dve.wait_ge(s_ez, t)
                    V.reduce_sum(esum[:, 0:H * n], e3, AX.X).then_inc(s_zsum, 1)
                    dve.wait_ge(s_zsum, t)
                    V.reciprocal(rsum[:, 0:H * n], esum[:, 0:H * n]).then_inc(s_zr, 1)
                    dve.wait_ge(s_zr, t)
                    V.tensor_tensor(e3, e3, rsum[:, 0:H * n].rearrange("p (a b) -> p a b", b=1).to_broadcast([P, H * n, F]),
                                    ALU.mult).then_inc(s_zn, 1)
                    dve.wait_ge(s_zn, t)
                    V.tensor_tensor(msg[b].rearrange("p f c -> p c f"), e4[:, :, 0, :], e4[:, :, 1, :],
                                    ALU.add).then_inc(s_msg, 1)
                    dve.wait_ge(s_msg, t)
                    V.scalar_tensor_tensor(msg[b][:, :, 0], run[1 - b][:, :, m_before - 1], cont[:, ds(k * CC + off, 1)],
                                           msg[b][:, :, 0], ALU.mult, ALU.add).then_inc(s_carried, 1)
                    dve.wait_ge(s_carried, t)
                    dve.wait_ge(s_contf, t)
                    V.tensor_tensor_scan(run[b][:].rearrange("p f c -> p (f c)"), cont_f[b][:].rearrange("p f c -> p (f c)"),
                                         msg[b].rearrange("p f c -> p (f c)"), 0.0, ALU.mult, ALU.add).then_inc(s_run, 1)
                    dve.wait_ge(s_run, t)
                    cl = closed[:, 0:F * n].rearrange("p (f c) -> p f c", c=n)
                    V.tensor_tensor(cl, run[b][:], close[:, cols].rearrange("p (a c) -> p a c", a=1).to_broadcast([P, F, n]),
                                    ALU.mult).then_inc(s_cl, 1)
                    dve.wait_ge(s_cl, t)
                    V.reduce_sum(closed_part[:], cl, AX.X).then_inc(s_cls, 1)
                    dve.wait_ge(s_cls, t)
                    V.tensor_tensor(closed_sum[:], closed_sum[:], closed_part[:], ALU.add).then_inc(s_fsum, 1)
                    if later(k):
                        dve.wait_ge(s_scat[b], 16 * n * k)
                    V.tensor_copy(ring[b][:], scat_idx[:, cols]).then_inc(s_scidx, 1)
                    for i, (c, m) in enumerate(UNITS[b]):
                        dve.wait_ge(s_ou, UPC * k + unit_no3[b, i] + 1)
                        V.tensor_tensor(rows[b][:, c:c + m, :], ps_b[:, 0:m * F].rearrange("p (c f) -> p c f", f=F),
                                        base[:, ds(k * CC + off + c, m), :], ALU.add).then_inc(s_row, 1)
            chunks(V, third)

            dve.wait_ge(s_fixt, 1)
            V.tensor_tensor_scan(left_sum[:, 1:P + 1], whole_row[:, 0, :], ps_row[0:F, 0:P], 0.0, ALU.mult, ALU.add).then_inc(s_fix, 1)
            dve.wait_ge(s_fixt, 2)
            dve.wait_ge(s_fsum, 2 * K)
            V.tensor_tensor(fix_in[:], ps_row[:, P:P + F], closed_sum[:], ALU.add).then_inc(s_fix, 1)
            dve.wait_ge(s_fixt, 3)
            V.tensor_copy(fix_t[:], ps_row[0:F, 2 * P:3 * P]).then_inc(s_fix, 1)
            dve.wait_ge(s_fixt, 4)
            V.tensor_tensor(fix_rows[:], ps_row[:, 3 * P:3 * P + F], base[:, 0, :], ALU.add).then_inc(s_fixs, 1)


_INS = ["x", "src", "dst", "edge_attr3_2x32", "L0_gnn_W1", "L0_gnn_b1", "L0_gnn_W2s", "L0_gnn_b2s",
        "L0_gnn_W2d", "L0_gnn_b2d", "L0_gnn_attn"]


def kernel(**inputs):
    import numpy as _np
    import concourse.bacc as _bacc
    from concourse import mybir as _mybir
    from concourse.bass_utils import run_bass_kernel_spmd as _run

    nc = _bacc.Bacc("TRN2", target_bir_lowering=False, num_devices=1)
    arrays, args = {}, []
    for name in _INS:
        a = _np.ascontiguousarray(inputs[name])
        arrays[f"in_{name}_dram"] = a
        args.append(nc.dram_tensor(f"in_{name}_dram", a.shape, _mybir.dt.from_np(a.dtype), kind="ExternalInput").ap())
    shape = inputs["x"].shape
    out = nc.dram_tensor("out_0_dram", shape, _mybir.dt.float32, kind="ExternalOutput").ap()
    gnn_kernel(nc, *args, out)
    r = _run(nc, [arrays], core_ids=[0])
    return r.results[0]["out_0_dram"]
```
